# Optimizing a Trainium2 kernel written in Bass

```python
import numpy as np
import jax
import jax.numpy as jnp

def _softmax(x, axis=-1):
    return jax.nn.softmax(x, axis=axis)

def _gelu(x):
    return jax.nn.gelu(x, approximate=True)

def _silu(x):
    return jax.nn.silu(x)

def _sigmoid(x):
    return jax.nn.sigmoid(x)

def _layernorm(x, axis=-1, eps=1e-05):
    m = jnp.mean(x, axis=axis, keepdims=True)
    v = jnp.var(x, axis=axis, keepdims=True)
    return (x - m) / jnp.sqrt(v + eps)

def _scatter_add(tgt, idx, src, axis=0):
    return tgt.at[idx].add(src)

def _segment_sum(src, seg, n):
    return jax.ops.segment_sum(src, seg, n)
kernel_name = 'mk_flamingo_gated_d2_seqx_r8_112fb4'

def setup_inputs(seed: int=0):
    np.random.seed(seed)
    _w = jnp.asarray

    def _rec_inputs():
        import jax
        import jax.numpy as jnp
        _rk = jax.random.key(seed)
        x = 7.22e-05 + 1 * jax.random.normal(jax.random.fold_in(_rk, 1), (64, 64, 128), jnp.float32)
        _lenS = 64 - jax.random.randint(jax.random.fold_in(_rk, 7), (64,), 0, max(1, 64 // 4) + 1, jnp.int32)
        _lenS2 = 64 - jax.random.randint(jax.random.fold_in(_rk, 8), (64,), 0, max(1, 64 // 4) + 1, jnp.int32)
        _ctx_1024P = jax.random.normal(jax.random.fold_in(_rk, 11), (64, 16, 128), jnp.float32)
        _ctx_1024c = jax.random.dirichlet(jax.random.fold_in(_rk, 511), 0.3 * jnp.ones((16,), jnp.float32), (64, 64))
        _ctx_1024t = jnp.einsum('bsk,bkd->bsd', _ctx_1024c, _ctx_1024P)
        _ctx_1024t = _ctx_1024t * jax.lax.rsqrt(jnp.mean(jnp.square(_ctx_1024t)) + 1e-12) * 0.953939
        ctx_1024 = 4.13588e-05 + 0.999923 * (_ctx_1024t + 0.3 * jax.random.normal(jax.random.fold_in(_rk, 611), (64, 64, 128), jnp.float32))
        _g = jax.random.normal(jax.random.fold_in(_rk, 9001), (2, 2), jnp.float32)
        _g = jnp.sign(_g) * jnp.maximum(jnp.abs(_g), 1.0) + (_g == 0) * 1.0
        g_xattn = _g[0]
        g_ffn = _g[1]
        return (x, ctx_1024, g_xattn, g_ffn)
    x, ctx_1024, g_xattn, g_ffn = _rec_inputs()

    def _L0_xattn_setup():
        import jax, jax.numpy as jnp
        import numpy as np
        import math
        DIM = 128
        HEADS = 16
        WINDOW = 32

        def _rope(x):
            b, s, d = x.shape
            half = d // 2
            inv_freq = 1.0 / 10000.0 ** (jnp.arange(half, dtype=jnp.float32) / half)
            ang = jnp.arange(s, dtype=jnp.float32)[:, None] * inv_freq[None, :]
            cos, sin = (jnp.cos(ang), jnp.sin(ang))
            x1, x2 = (x[..., :half], x[..., half:])
            return jnp.concatenate([x1 * cos - x2 * sin, x1 * sin + x2 * cos], axis=-1)
        key = jax.random.key(seed)
        ks = jax.random.split(key, 8)
        d = DIM
        q = jax.random.normal(ks[0], (2, 512, d), dtype=jnp.float32)
        k = jax.random.normal(ks[1], (2, 512, d), dtype=jnp.float32)
        v = jax.random.normal(ks[2], (2, 512, d), dtype=jnp.float32)
        wq = jax.random.normal(ks[3], (d, d), dtype=jnp.float32) * 0.02
        wk = jax.random.normal(ks[4], (d, d), dtype=jnp.float32) * 0.02
        wv = jax.random.normal(ks[5], (d, d), dtype=jnp.float32) * 0.02
        wo_w = jax.random.normal(ks[6], (d, d), dtype=jnp.float32) * 0.02
        wo_b = jnp.zeros((d,), dtype=jnp.float32)
        return {'q': q, 'k': k, 'v': v, 'wq': wq, 'wk': wk, 'wv': wv, 'wo_w': wo_w, 'wo_b': wo_b}
    _L0_xattn_all = _L0_xattn_setup()
    _L0_xattn_in = {k: v for k, v in _L0_xattn_all.items() if k in ('wq', 'wk', 'wv', 'wo_w', 'wo_b')}
    del _L0_xattn_all

    def _L0_ffn_setup():
        import jax, jax.numpy as jnp
        import numpy as np
        H = 128
        I = 88
        E = 64
        TOP_K = 8
        NG = 8
        TOPK_GROUP = 4
        N_SHARED = 2
        ROUTED_SCALE = 2.5
        S_I = I * N_SHARED

        def _route(x, gate_w, gate_bias):
            T = x.shape[0]
            logits = x @ gate_w.T
            scores = jax.nn.sigmoid(logits)
            scores_for_choice = scores + gate_bias[None, :]
            grp = scores_for_choice.reshape(T, NG, E // NG)
            group_scores = jnp.sum(jax.lax.top_k(grp, 2)[0], axis=-1)
            _, gidx = jax.lax.top_k(group_scores, TOPK_GROUP)
            gmask = jnp.zeros((T, NG), dtype=scores.dtype).at[jnp.arange(T)[:, None], gidx].set(1.0)
            emask = jnp.repeat(gmask, E // NG, axis=1)
            masked = jnp.where(emask > 0, scores_for_choice, 0.0)
            _, topk_idx = jax.lax.top_k(masked, TOP_K)
            topk_w = jnp.take_along_axis(scores, topk_idx, axis=1)
            topk_w = topk_w / (jnp.sum(topk_w, axis=-1, keepdims=True) + 1e-20)
            topk_w = topk_w * ROUTED_SCALE
            rw = jnp.zeros((T, E), dtype=scores.dtype).at[jnp.arange(T)[:, None], topk_idx].add(topk_w)
            return rw

        def _mlp(x, gw, uw, dw):
            return jax.nn.silu(x @ gw.T) * (x @ uw.T) @ dw.T
        key = jax.random.key(seed)
        ks = jax.random.split(key, 10)
        sc = 0.02
        return {'hidden_states': jax.random.normal(ks[0], (1, 128, H), dtype=jnp.float32), 'gate_w': sc * jax.random.normal(ks[1], (E, H), dtype=jnp.float32), 'gate_bias': sc * jax.random.normal(ks[2], (E,), dtype=jnp.float32), 'Wg': sc * jax.random.normal(ks[3], (E, I, H), dtype=jnp.float32), 'Wu': sc * jax.random.normal(ks[4], (E, I, H), dtype=jnp.float32), 'Wd': sc * jax.random.normal(ks[5], (E, H, I), dtype=jnp.float32), 'Sg': sc * jax.random.normal(ks[6], (S_I, H), dtype=jnp.float32), 'Su': sc * jax.random.normal(ks[7], (S_I, H), dtype=jnp.float32), 'Sd': sc * jax.random.normal(ks[8], (H, S_I), dtype=jnp.float32)}
    _L0_ffn_all = _L0_ffn_setup()
    _L0_ffn_in = {k: v for k, v in _L0_ffn_all.items() if k in ('gate_w', 'gate_bias', 'Wg', 'Wu', 'Wd', 'Sg', 'Su', 'Sd')}
    del _L0_ffn_all

    def _L1_xattn_setup():
        import jax, jax.numpy as jnp
        import numpy as np
        D_MODEL = 128
        H = 16
        D_K = D_MODEL // H

        def _split_heads(x, B):
            return x.reshape(B, -1, H, D_K).transpose(0, 2, 1, 3)
        key = jax.random.key(seed)
        ks = jax.random.split(key, 11)
        B, S = (4, 256)
        scale = 1.0 / np.sqrt(D_MODEL)
        inp = {'q': jax.random.normal(ks[0], (B, S, D_MODEL), jnp.float32), 'k': jax.random.normal(ks[1], (B, S, D_MODEL), jnp.float32), 'v': jax.random.normal(ks[2], (B, S, D_MODEL), jnp.float32), 'W_q': jax.random.normal(ks[3], (D_MODEL, D_MODEL), jnp.float32) * scale, 'b_q': jnp.zeros((D_MODEL,), jnp.float32), 'W_k': jax.random.normal(ks[4], (D_MODEL, D_MODEL), jnp.float32) * scale, 'b_k': jnp.zeros((D_MODEL,), jnp.float32), 'W_v': jax.random.normal(ks[5], (D_MODEL, D_MODEL), jnp.float32) * scale, 'b_v': jnp.zeros((D_MODEL,), jnp.float32), 'W_o': jax.random.normal(ks[6], (D_MODEL, D_MODEL), jnp.float32) * scale, 'b_o': jnp.zeros((D_MODEL,), jnp.float32)}
        return inp
    _L1_xattn_all = _L1_xattn_setup()
    _L1_xattn_in = {k: v for k, v in _L1_xattn_all.items() if k in ('W_q', 'b_q', 'W_k', 'b_k', 'W_v', 'b_v', 'W_o', 'b_o')}
    del _L1_xattn_all

    def _L1_ffn_setup():
        import jax, jax.numpy as jnp
        import numpy as np
        B, S, H, F, E, K = (4, 512, 128, 512, 8, 2)
        key = jax.random.key(seed)
        ks = jax.random.split(key, 4)
        x = jax.random.normal(ks[0], (B, S, H), dtype=jnp.float32)
        Wg = jax.random.normal(ks[1], (H, E), dtype=jnp.float32) * (1.0 / np.sqrt(H))
        W1 = jax.random.normal(ks[2], (E, H, F), dtype=jnp.float32) * (1.0 / np.sqrt(H))
        b1 = jnp.zeros((E, F), dtype=jnp.float32)
        W2 = jax.random.normal(ks[3], (E, F, H), dtype=jnp.float32) * (1.0 / np.sqrt(F))
        b2 = jnp.zeros((E, H), dtype=jnp.float32)
        return {'x': x, 'Wg': Wg, 'W1': W1, 'b1': b1, 'W2': W2, 'b2': b2}
    _L1_ffn_all = _L1_ffn_setup()
    _L1_ffn_in = {k: v for k, v in _L1_ffn_all.items() if k in ('Wg', 'W1', 'b1', 'W2', 'b2')}
    del _L1_ffn_all
    return {'x': x, 'ctx_1024': ctx_1024, 'g_xattn': g_xattn, 'g_ffn': g_ffn, 'L0_xattn_wq': _L0_xattn_in['wq'], 'L0_xattn_wk': _L0_xattn_in['wk'], 'L0_xattn_wv': _L0_xattn_in['wv'], 'L0_xattn_wo_w': _L0_xattn_in['wo_w'], 'L0_xattn_wo_b': _L0_xattn_in['wo_b'], 'L0_ffn_gate_w': _L0_ffn_in['gate_w'], 'L0_ffn_gate_bias': _L0_ffn_in['gate_bias'], 'L0_ffn_Wg': _L0_ffn_in['Wg'], 'L0_ffn_Wu': _L0_ffn_in['Wu'], 'L0_ffn_Wd': _L0_ffn_in['Wd'], 'L0_ffn_Sg': _L0_ffn_in['Sg'], 'L0_ffn_Su': _L0_ffn_in['Su'], 'L0_ffn_Sd': _L0_ffn_in['Sd'], 'L1_xattn_W_q': _L1_xattn_in['W_q'], 'L1_xattn_b_q': _L1_xattn_in['b_q'], 'L1_xattn_W_k': _L1_xattn_in['W_k'], 'L1_xattn_b_k': _L1_xattn_in['b_k'], 'L1_xattn_W_v': _L1_xattn_in['W_v'], 'L1_xattn_b_v': _L1_xattn_in['b_v'], 'L1_xattn_W_o': _L1_xattn_in['W_o'], 'L1_xattn_b_o': _L1_xattn_in['b_o'], 'L1_ffn_Wg': _L1_ffn_in['Wg'], 'L1_ffn_W1': _L1_ffn_in['W1'], 'L1_ffn_b1': _L1_ffn_in['b1'], 'L1_ffn_W2': _L1_ffn_in['W2'], 'L1_ffn_b2': _L1_ffn_in['b2']}

def reference(x, ctx_1024, g_xattn, g_ffn, L0_xattn_wq, L0_xattn_wk, L0_xattn_wv, L0_xattn_wo_w, L0_xattn_wo_b, L0_ffn_gate_w, L0_ffn_gate_bias, L0_ffn_Wg, L0_ffn_Wu, L0_ffn_Wd, L0_ffn_Sg, L0_ffn_Su, L0_ffn_Sd, L1_xattn_W_q, L1_xattn_b_q, L1_xattn_W_k, L1_xattn_b_k, L1_xattn_W_v, L1_xattn_b_v, L1_xattn_W_o, L1_xattn_b_o, L1_ffn_Wg, L1_ffn_W1, L1_ffn_b1, L1_ffn_W2, L1_ffn_b2):
    import jax
    import jax.numpy as jnp

    def _L0_xattn_ref(q, k, v, wq, wk, wv, wo_w, wo_b):
        import jax, jax.numpy as jnp
        import numpy as np
        import math
        DIM = 128
        HEADS = 16
        WINDOW = 32

        def _rope(x):
            b, s, d = x.shape
            half = d // 2
            inv_freq = 1.0 / 10000.0 ** (jnp.arange(half, dtype=jnp.float32) / half)
            ang = jnp.arange(s, dtype=jnp.float32)[:, None] * inv_freq[None, :]
            cos, sin = (jnp.cos(ang), jnp.sin(ang))
            x1, x2 = (x[..., :half], x[..., half:])
            return jnp.concatenate([x1 * cos - x2 * sin, x1 * sin + x2 * cos], axis=-1)
        b, s, d = q.shape
        h, W = (HEADS, WINDOW)
        dk = d // h
        B = W
        nb = s // B
        qp = _rope(jnp.einsum('bsd,ed->bse', q, wq))
        kp = _rope(jnp.einsum('bsd,ed->bse', k, wk))
        vp = jnp.einsum('bsd,ed->bse', v, wv)
        qh = qp.reshape(b, s, h, dk).transpose(0, 2, 1, 3)
        kh = kp.reshape(b, s, h, dk).transpose(0, 2, 1, 3)
        vh = vp.reshape(b, s, h, dk).transpose(0, 2, 1, 3)
        kpad = jnp.pad(kh, ((0, 0), (0, 0), (B, B), (0, 0)))
        vpad = jnp.pad(vh, ((0, 0), (0, 0), (B, B), (0, 0)))
        kblk = kpad.reshape(b, h, nb + 2, B, dk)
        vblk = vpad.reshape(b, h, nb + 2, B, dk)
        kband = jnp.concatenate([kblk[:, :, i:i + nb] for i in range(3)], axis=3)
        vband = jnp.concatenate([vblk[:, :, i:i + nb] for i in range(3)], axis=3)
        qb = qh.reshape(b, h, nb, B, dk)
        scores = jnp.einsum('bhnqd,bhnkd->bhnqk', qb, kband) * math.sqrt(dk)
        n_idx = jnp.arange(nb)[:, None, None]
        qi = jnp.arange(B)[None, :, None]
        ki = jnp.arange(3 * B)[None, None, :]
        kpos = (n_idx - 1) * B + ki
        rel = ki - B - qi
        valid = (rel >= -W) & (rel <= W) & (kpos >= 0) & (kpos < s)
        neg = jnp.asarray(jnp.finfo(scores.dtype).min, scores.dtype)
        scores = jnp.where(valid[None, None], scores, neg)
        attn = jax.nn.softmax(scores, axis=-1)
        out = jnp.einsum('bhnqk,bhnkd->bhnqd', attn, vband)
        out = out.reshape(b, h, s, dk).transpose(0, 2, 1, 3).reshape(b, s, d)
        return jnp.einsum('bsd,ed->bse', out, wo_w) + wo_b

    def _L0_ffn_ref(hidden_states, gate_w, gate_bias, Wg, Wu, Wd, Sg, Su, Sd):
        import jax, jax.numpy as jnp
        import numpy as np
        H = 128
        I = 88
        E = 64
        TOP_K = 8
        NG = 8
        TOPK_GROUP = 4
        N_SHARED = 2
        ROUTED_SCALE = 2.5
        S_I = I * N_SHARED

        def _route(x, gate_w, gate_bias):
            T = x.shape[0]
            logits = x @ gate_w.T
            scores = jax.nn.sigmoid(logits)
            scores_for_choice = scores + gate_bias[None, :]
            grp = scores_for_choice.reshape(T, NG, E // NG)
            group_scores = jnp.sum(jax.lax.top_k(grp, 2)[0], axis=-1)
            _, gidx = jax.lax.top_k(group_scores, TOPK_GROUP)
            gmask = jnp.zeros((T, NG), dtype=scores.dtype).at[jnp.arange(T)[:, None], gidx].set(1.0)
            emask = jnp.repeat(gmask, E // NG, axis=1)
            masked = jnp.where(emask > 0, scores_for_choice, 0.0)
            _, topk_idx = jax.lax.top_k(masked, TOP_K)
            topk_w = jnp.take_along_axis(scores, topk_idx, axis=1)
            topk_w = topk_w / (jnp.sum(topk_w, axis=-1, keepdims=True) + 1e-20)
            topk_w = topk_w * ROUTED_SCALE
            rw = jnp.zeros((T, E), dtype=scores.dtype).at[jnp.arange(T)[:, None], topk_idx].add(topk_w)
            return rw

        def _mlp(x, gw, uw, dw):
            return jax.nn.silu(x @ gw.T) * (x @ uw.T) @ dw.T
        B, S, _ = hidden_states.shape
        x = hidden_states.reshape(B * S, H)
        rw = _route(x, gate_w, gate_bias)
        expert_out = jax.vmap(lambda gw_, uw_, dw_: _mlp(x, gw_, uw_, dw_))(Wg, Wu, Wd)
        routed = jnp.einsum('eth,te->th', expert_out, rw)
        shared = _mlp(x, Sg, Su, Sd)
        out = (routed + shared).reshape(B, S, H)
        return out

    def _L1_xattn_ref(q, k, v, W_q, b_q, W_k, b_k, W_v, b_v, W_o, b_o):
        import jax, jax.numpy as jnp
        import numpy as np
        D_MODEL = 128
        H = 16
        D_K = D_MODEL // H

        def _split_heads(x, B):
            return x.reshape(B, -1, H, D_K).transpose(0, 2, 1, 3)
        B = q.shape[0]
        qh = _split_heads(q @ W_q + b_q, B)
        kh = _split_heads(k @ W_k + b_k, B)
        vh = _split_heads(v @ W_v + b_v, B)
        scores = jnp.einsum('bhsd,bhtd->bhst', qh, kh) / jnp.sqrt(jnp.float32(D_K))
        attn = jax.nn.softmax(scores, axis=-1)
        out = jnp.einsum('bhst,bhtd->bhsd', attn, vh)
        out = out.transpose(0, 2, 1, 3).reshape(B, -1, H * D_K)
        return out @ W_o + b_o

    def _L1_ffn_ref(x, Wg, W1, b1, W2, b2):
        import jax, jax.numpy as jnp
        import numpy as np
        B, S, H, F, E, K = (4, 512, 128, 512, 8, 2)
        b, s, h = x.shape
        e = W1.shape[0]
        xf = x.reshape(-1, h)
        logits = xf @ Wg
        top_vals, top_idx = jax.lax.top_k(logits, K)
        gate_w = jax.nn.softmax(top_vals, axis=-1)
        comb = jnp.sum(gate_w[..., None] * jax.nn.one_hot(top_idx, e, dtype=xf.dtype), axis=1)
        out = jnp.zeros_like(xf)
        for ei in range(e):
            hdd = jax.nn.gelu(xf @ W1[ei] + b1[ei])
            y = hdd @ W2[ei] + b2[ei]
            out = out + comb[:, ei:ei + 1] * y
        return out.reshape(b, s, h)
    x = x + jnp.tanh(g_xattn[0]) * _L0_xattn_ref(_layernorm(x, axis=-1), ctx_1024, ctx_1024, L0_xattn_wq, L0_xattn_wk, L0_xattn_wv, L0_xattn_wo_w, L0_xattn_wo_b)
    x = x + jnp.tanh(g_ffn[0]) * _L0_ffn_ref(_layernorm(x, axis=-1), L0_ffn_gate_w, L0_ffn_gate_bias, L0_ffn_Wg, L0_ffn_Wu, L0_ffn_Wd, L0_ffn_Sg, L0_ffn_Su, L0_ffn_Sd)
    x = x + jnp.tanh(g_xattn[1]) * _L1_xattn_ref(_layernorm(x, axis=-1), ctx_1024, ctx_1024, L1_xattn_W_q, L1_xattn_b_q, L1_xattn_W_k, L1_xattn_b_k, L1_xattn_W_v, L1_xattn_b_v, L1_xattn_W_o, L1_xattn_b_o)
    x = x + jnp.tanh(g_ffn[1]) * _L1_ffn_ref(_layernorm(x, axis=-1), L1_ffn_Wg, L1_ffn_W1, L1_ffn_b1, L1_ffn_W2, L1_ffn_b2)
    return x

_drawn_inputs = setup_inputs


def setup_inputs(seed=0):
    import zlib

    import numpy as np

    out = dict(_drawn_inputs(seed))
    spreads = {'g_ffn': (-1.0, 0.6),
     'L0_xattn_wo_b': (0.0, 0.1),
     'L1_xattn_b_q': (0.0, 0.1),
     'L1_xattn_b_k': (0.0, 0.8),
     'L1_xattn_b_v': (0.0, 0.1),
     'L1_xattn_b_o': (0.0, 0.1),
     'L1_ffn_b1': (0.0, 0.1),
     'L1_ffn_b2': (0.0, 0.1)}
    factors = {'L0_xattn_wq': 4.543,
     'L0_xattn_wk': 4.352,
     'L0_ffn_gate_w': 5.352,
     'L0_ffn_gate_bias': 6.285,
     'L0_ffn_Wg': 4.138,
     'L0_ffn_Wu': 4.61,
     'L0_ffn_Wd': 4.51,
     'L0_ffn_Sg': 3.847,
     'L0_ffn_Su': 3.559,
     'L0_ffn_Sd': 3.697}
    for name, (base, spread) in spreads.items():
        noise = np.random.default_rng([zlib.crc32(name.encode()), seed]).standard_normal(out[name].shape)
        drawn = base * np.exp(spread * noise) if base else spread * noise
        out[name] = jnp.asarray(drawn.astype(out[name].dtype))
    for name, factor in factors.items():
        out[name] = (out[name] * factor).astype(out[name].dtype)
    return out
```

```python
import numpy as np
from contextlib import ExitStack

import concourse.bass as bass
from concourse import mybir

ALU = mybir.AluOpType
ACT = mybir.ActivationFunctionType
AX = mybir.AxisListType
F32 = mybir.dt.float32
F32R = mybir.dt.float32r
BF16 = mybir.dt.bfloat16

P = 128
BATCH, SEQ, D = 64, 64, 128
TOK = BATCH * SEQ
HEADS, HD = 16, 8
EPS = 1e-5
MASKED = -1e30

GB = 4
GTOK = GB * SEQ
GROUPS = TOK // GTOK
STRIPS = 4
VW = 34

E0, I0, TOPK0, NG0, TOPG0 = 64, 88, 8, 8, 4
SHARED = 176
RSCALE = 2.5
ROUTED0 = E0 * I0
ROWS0 = ROUTED0 + SHARED
E1, F1 = 8, 512
ROWS1 = E1 * F1
FTOK = 512
FGROUPS = TOK // FTOK

C_ID, C_ID2, C_VM, C_JM, C_HM, C_COS, C_SIN, C_BAND, C_TRI, C_END = (
    0, 128, 192, 224, 226, 230, 294, 358, 422, 486)


def constants():
    c = np.zeros((P, C_END), np.float32)
    row = np.arange(P)
    c[:, C_ID:C_ID2] = np.eye(P)
    c[:, C_ID2:C_VM] = (row % 64)[:, None] == np.arange(64)
    c[:, C_VM:C_JM] = (row // 64)[:, None] == (np.arange(32) // 16)
    c[:, C_JM:C_HM] = (row // 64)[:, None] == np.arange(2)
    c[:, C_HM:C_COS] = ((row % 32) // HD)[:, None] == np.arange(4)
    half = D // 2
    inv = np.float32(1.0) / np.float32(10000.0) ** (np.arange(half, dtype=np.float32) / np.float32(half))
    ang = np.arange(SEQ, dtype=np.float32)[:, None] * inv[None, :]
    cos, sin = np.cos(ang).T, np.sin(ang).T
    c[:, C_COS:C_SIN] = np.concatenate([cos, cos])
    c[:half, C_SIN:C_BAND] -= sin
    c[half:, C_SIN:C_BAND] += sin
    q, k = (row % 64)[:, None], np.arange(64)[None, :]
    c[:, C_BAND:C_TRI] = np.where(abs(q - k) <= 32, 0.0, MASKED)
    i, j = np.arange(8)[:, None], np.arange(8)[None, :]
    c[:, C_TRI:C_END] = (j < i).reshape(1, 64)
    return c


def spread_rows(experts, rows, total):
    owner = np.arange(total) // rows
    one = (np.arange(experts)[:, None] == owner[None, :]).astype(np.float32)
    return np.concatenate([one, one])


def build(nc, A, out):
    x_dram = A["x"].rearrange("b s d -> (b s) d").rearrange("(t p) d -> p t d", p=P)
    out_dram = out.rearrange("b s d -> (b s) d").rearrange("(t p) d -> p t d", p=P)

    with ExitStack() as ctx:
        def sb(name, shape, dt=F32):
            return ctx.enter_context(nc.sbuf_tensor(name, shape, dt))

        def sem(name):
            return ctx.enter_context(nc.semaphore(name))

        bank = [ctx.enter_context(nc.psum_tensor(f"bank{i}", [P, 512], F32)) for i in range(8)]
        score = bank[0:4]
        w0, w1, w2, w3 = bank[4:8]

        x = sb("x", [P, TOK])
        xn2T = sb("xn2T", [P, TOK])
        rwT = sb("rwT", [P, TOK], F32R)
        cst = sb("cst", [P, C_END])
        idr = sb("idr", [P, P], F32R)
        band = sb("band", [P, 64], BF16)
        idb = sb("idb", [P, P], BF16)
        wup = sb("wup", [P, 2 * ROWS0])
        wdn = sb("wdn", [P, 46 * P])
        sel = sb("sel", [P, ROUTED0], F32R)
        sel1 = sel[0:2 * E1, 0:E1 * P]
        gates = sb("gates", [P, 4])
        mhalf = sb("mhalf", [P, 2])
        idle = sb("idle", [P, 48])

        wq = sb("wq", [P, 2, 2 * P])
        wv = sb("wv", [P, P])
        wo = sb("wo", [P, P])
        wr = sb("wr", [P, E0])
        brow = sb("brow", [P, 3, P])
        bcol = sb("bcol", [P, 2])
        bq4 = sb("bq4", [P, 4])
        b1 = sb("b1", [P, 32])
        b2 = sb("b2", [2 * E1, P])
        gbo = sb("gbo", [P, P])
        bvm = sb("bvm", [P, P])

        ctxT = sb("ctxT", [P, 2, GB, 2, SEQ])
        st = sb("st", [P, 2, 2, 6])
        mv = sb("mv", [P, 2, 2, 2])
        ve = sb("ve", [P, 2, 2])
        rs = sb("rs", [P, 2, 2])
        xn = sb("xn", [P, 2, 2, P])
        xnT = sb("xnT", [P, 2, GTOK])
        rope = sb("rope", [P, 4, GTOK])
        qr = sb("qr", [P, GTOK])
        qm = sb("qm", [P, 2, GB, 4, SEQ])
        kr = sb("kr", [P, 2, GTOK])
        vm = sb("vm", [P, 2, GB, STRIPS, VW])
        nmax = sb("nmax", [P, 4, 8], F32R)
        work = sb("work", [P, 4, 512])
        work2 = sb("work2", [P, 3, 512])
        rden = sb("rden", [P, 2, GB, 2])
        rdm = sb("rdm", [P, 2, GB, 2, 2])
        on = sb("on", [P, 2, GB, P])
        aT = sb("aT", [P, GTOK])
        xb = sb("xb", [P, 2, GTOK])
        st2 = sb("st2", [P, 2, 6])
        mv2 = sb("mv2", [P, 2, 2])
        ve2 = sb("ve2", [P, 2])
        rs2 = sb("rs2", [P, 2])
        xn2 = sb("xn2", [P, 2, P])
        ysb = sb("ysb", [P, FTOK])
        sg = sb("sg", [P, 2 * E0])
        sc = sb("sc", [P, 2 * E0])
        choice = sb("choice", [P, 2 * E0])
        gtop = sb("gtop", [P, 16, 8])
        gsum = sb("gsum", [P, 16])
        cmp = sb("cmp", [P, 2, P])
        rank = sb("rank", [P, 16])
        masked = sb("masked", [P, 2 * E0])
        top8 = sb("top8", [P, 2, 8])
        rest = sb("rest", [P, 2 * E0])
        wsel = sb("wsel", [P, 2 * E0])
        wsum = sb("wsum", [P, 2])
        rw = sb("rw", [P, 4 * E0])
        rwr = sb("rwr", [P, 2 * E0], F32R)

        s_const = sem("s_const"); s_x = sem("s_x"); s_ffw = sem("s_ffw"); s_sel = sem("s_sel")
        s_setup = sem("s_setup"); s_half = sem("s_half"); s_ones = sem("s_ones")
        s_out = sem("s_out")

        def layer_semaphores(L):
            names = (
                "weights", "tanh", "prep",
                "stats", "varp", "rstd", "xn", "xt", "xt_copied", "qp", "q_read", "q_roped", "q_masked",
                "kp", "k_read", "k_done", "vp", "v_masked", "v_done",
                "scores", "max_done", "shifted", "probs", "pt", "pt_copied", "op", "rden", "rdm", "o_done",
                "at", "at_copied", "xb", "y", "resid", "stats2", "varp2", "rstd2", "xn2", "x2t", "x2t_copied",
                "x2_kept", "lg", "lg_read", "route_v", "route_p", "p2v", "v2p", "rt", "rt_copied", "a2v", "v2a", "chain",
                "gate", "up", "spread", "act", "prod", "hid", "down", "y_copied", "yt", "x_done")
            S = {name: sem(f"{name}{L}") for name in names}
            S["ctx"] = [sem(f"ctx_loaded{L}_{i}") for i in range(2)]
            if L == 1:
                S["q_read"], S["k_read"] = S["q_masked"], S["k_done"]
            return S

        layers = [layer_semaphores(0), layer_semaphores(1)]

        block = ctx.enter_context(nc.Block())

        def first(value, n):
            return isinstance(value, int) and value == n

        held = {}

        def hold(eng, semaphore, value):
            eng.wait_ge(semaphore, value)
            if not isinstance(value, int):
                n = held.setdefault((eng.engine, semaphore.name), len(held))
                if eng.engine == mybir.EngineType.Pool:
                    eng.tensor_tensor(idle[:, n:n + 1], mhalf[:, 0:1], mhalf[:, 1:2], ALU.add)
                else:
                    eng.tensor_copy(idle[:, n:n + 1], cst[:, 0:1])

        def slots(eng, step):
            for j in range(4):
                step(j, j % 2, True, j >= 1, j >= 2, j >= 3)
            with eng.Fori(0, (GROUPS - 6) // 2) as i:
                for h in range(2):
                    step(i * 2 + 4 + h, h, True, True, True, True)
            for j in (GROUPS - 2, GROUPS - 1):
                step(j, j % 2, True, True, True, True)
            step(GROUPS, 0, False, True, True, True)
            step(GROUPS + 1, 1, False, False, True, True)
            step(GROUPS + 2, 0, False, False, False, True)

        @block.sync
        def _(sp):
            sp.dma_start(cst[:], A["cst"]).then_inc(s_const, 16)
            S = layers[0]

            def small(L, S):
                pre = f"L{L}_"
                sp.dma_start(gates[:, 0:2], A["g_xattn"].rearrange("(a n) -> a n", a=1).to_broadcast([P, 2])).then_inc(S["weights"], 16)
                sp.dma_start(gates[:, 2:4], A["g_ffn"].rearrange("(a n) -> a n", a=1).to_broadcast([P, 2])).then_inc(S["weights"], 16)
                for n, s in enumerate(("q", "k")):
                    src = A[pre + "w" + s]
                    sp.dma_start(wq[:, n, 0:src.shape[1]], src).then_inc(S["weights"], 16)
                sp.dma_start(wv[:], A[pre + "wv"]).then_inc(S["weights"], 16)
                sp.dma_start(wo[:], A[pre + "wo"]).then_inc(S["weights"], 16)
                r = A[pre + "router"]
                sp.dma_start(wr[:, 0:r.shape[1]], r).then_inc(S["weights"], 16)
                sp.dma_start(brow[:, 0, :], A[pre + "bo"].rearrange("(a n) -> a n", a=1).to_broadcast([P, P])).then_inc(S["weights"], 16)
                if L == 0:
                    sp.dma_start(brow[:, 1, 0:E0], A["L0_ffn_gate_bias"].rearrange("(a n) -> a n", a=1).to_broadcast([P, E0])).then_inc(S["weights"], 16)
                else:
                    sp.dma_start(brow[:, 1, :], A["L1_bv"].rearrange("(a n) -> a n", a=1).to_broadcast([P, P])).then_inc(S["weights"], 16)
                    sp.dma_start(bcol[:, 0:1], A["L1_bq"].rearrange("(n a) -> n a", a=1)).then_inc(S["weights"], 16)
                    sp.dma_start(bcol[:, 1:2], A["L1_bk"].rearrange("(n a) -> n a", a=1)).then_inc(S["weights"], 16)

            small(0, layers[0])
            for t in range(0, 32, 8):
                sp.dma_start(x[:, t * P:(t + 8) * P].rearrange("p (t d) -> p t d", d=P), x_dram[:, t:t + 8, :]).then_inc(s_x, 16)
            sp.dma_start(wup[:, 0:ROWS0], A["gate0"]).then_inc(s_ffw, 16)
            sp.dma_start(wup[:, ROWS0:], A["up0"]).then_inc(s_ffw, 16)
            sp.dma_start(wdn[:, 0:44 * P].rearrange("p (c d) -> p c d", d=P),
                         A["down0"][0:ROUTED0, :].rearrange("(c p) d -> p c d", p=P)).then_inc(s_ffw, 16)
            sp.dma_start(wdn[0:SHARED // 2, 44 * P:46 * P].rearrange("p (c d) -> p c d", d=P),
                         A["down0"][ROUTED0:ROWS0, :].rearrange("(c p) d -> p c d", p=SHARED // 2)).then_inc(s_ffw, 16)
            sp.wait_ge(layers[0]["x_done"], FGROUPS)
            small(1, layers[1])
            sp.dma_start(wup[:, 0:ROWS1], A["w1"]).then_inc(s_ffw, 16)
            sp.dma_start(wdn[:, 0:32 * P].rearrange("p (c d) -> p c d", d=P),
                         A["w2"].rearrange("(c p) d -> p c d", p=P)).then_inc(s_ffw, 16)
            sp.dma_start(b1[:], A["b1"]).then_inc(s_ffw, 16)
            for h in range(2):
                sp.dma_start(b2[h * E1:(h + 1) * E1, :], A["L1_ffn_b2"]).then_inc(s_ffw, 16)
            sp.wait_ge(layers[1]["x_done"], FGROUPS)
            sp.dma_start(out_dram, x[:].rearrange("p (t d) -> p t d", d=P)).then_inc(s_out, 16)
            sp.wait_ge(s_out, 16)

        N_SMALL = [9 * 16, 11 * 16]

        @block.tensor
        def _(pe):
            ident = cst[:, C_ID:C_ID + P]

            def attention(L):
                S = layers[L]
                pe.wait_ge(s_setup, 3)
                pe.wait_ge(S["weights"], N_SMALL[L])
                if L:
                    pe.wait_ge(layers[0]["x_done"], FGROUPS)

                def step(j, par, f, m, b, r):
                    fp, mp = par, 1 - par
                    M, B, R = j - 1, j - 2, j - 3

                    def scores(u):
                        if u == 0:
                            pe.wait_ge(S["k_done"], M + 1)
                            pe.wait_ge(S["q_masked"], M + 1)
                        if not first(j, 1):
                            pe.wait_ge(S["probs"], M * 4 + (u - 3))
                        rows = slice(32 * u, 32 * u + 32)
                        for bb in range(GB):
                            for p in range(2):
                                c = (bb * 2 + p) * SEQ
                                mm = pe.matmul(score[u][:, c:c + SEQ], qm[rows, mp, bb, 2 * p:2 * p + 2, :],
                                               kr[rows, mp, bb * SEQ:(bb + 1) * SEQ],
                                               start=(bb == 0 and p == 0), stop=False, skip_group_check=True)
                        if L == 0:
                            mm = pe.matmul(score[u][:, :], idb[:], band[:].unsqueeze(1).to_broadcast([P, 8, 64]),
                                           start=False, stop=False, skip_group_check=True)
                        mm.then_inc(S["scores"], 1)

                    def shift(u):
                        pe.wait_ge(S["max_done"], M * 4 + (u + 1))
                        pe.matmul(score[u][:, :], idr[:], nmax[:, u, :].unsqueeze(2).to_broadcast([P, 8, 64]),
                                  start=False, stop=True, skip_group_check=True).then_inc(S["shifted"], 1)

                    def turn(u):
                        pe.wait_ge(S["probs"], M * 4 + (u + 1))
                        w = (w0, w1)[u % 2]
                        if u == 0:
                            if f:
                                pe.wait_ge(S["xt_copied"], j + 1)
                            else:
                                pe.wait_ge(S["v_masked"], GROUPS)
                        if u == 1 and b:
                            pe.wait_ge(S["resid"], B + 1)
                        if u == 2:
                            pe.wait_ge(S["pt_copied"], M * 4 + 1)
                        if u == 3:
                            if b:
                                pe.wait_ge(S["lg_read"], B + 1)
                            else:
                                pe.wait_ge(S["pt_copied"], M * 4 + 2)
                        for bb in range(GB):
                            mm = pe.transpose(w[:, bb * P:(bb + 1) * P], work[:, u, bb * P:(bb + 1) * P], ident)
                        mm.then_inc(S["pt"], 1)

                    def values(u):
                        pe.wait_ge(S["pt_copied"], M * 4 + (u + 1))
                        w = (w3, w2)[u % 2]
                        if u == 0:
                            pe.wait_ge(S["v_done"] if L else S["v_masked"], M + 1)
                            if r:
                                pe.wait_ge(S["rt_copied"], R + 1)
                            elif b:
                                pe.wait_ge(S["o_done"], M * 4 - 1)
                            else:
                                pe.wait_ge(S["k_read"], M + 1)
                        if u == 1:
                            if b:
                                pe.wait_ge(S["x2t_copied"], B + 1)
                            else:
                                pe.wait_ge(S["q_read"], j + 1)
                        if u == 2:
                            if f:
                                pe.wait_ge(S["k_read"], j + 1)
                            else:
                                pe.wait_ge(S["o_done"], M * 4 + 1)
                        if u == 3:
                            pe.wait_ge(S["o_done"], M * 4 + 2)
                        for bb in range(GB):
                            mm = pe.matmul(w[:, bb * VW:(bb + 1) * VW], work2[:, u % 2, bb * P:(bb + 1) * P],
                                           vm[:, mp, bb, u, :], start=True, stop=True)
                        mm.then_inc(S["op"], 1)

                    def turn_x():
                        pe.wait_ge(S["xn"], j + 1)
                        if not first(j, 0):
                            pe.wait_ge(S["v_masked"], j)
                        for t in range(2):
                            mm = pe.transpose(w0[:, t * P:(t + 1) * P], xn[:, fp, t, :], ident)
                        mm.then_inc(S["xt"], 1)

                    def project(n, w, rhs, done):
                        for h in range(2 - L):
                            mm = pe.matmul(w[:, h * GTOK:(h + 1) * GTOK], wq[:, n, h * P:(h + 1) * P], rhs,
                                           start=True, stop=True)
                        mm.then_inc(done, 1)

                    def project_q():
                        if b:
                            pe.wait_ge(S["at_copied"], B + 1)
                        elif m:
                            pe.wait_ge(S["q_read"], j)
                        pe.wait_ge(S["xt_copied"], j + 1)
                        project(0, w2, xnT[:, fp, :], S["qp"])

                    def project_k():
                        if m:
                            pe.wait_ge(S["o_done"], M * 4 + 1)
                        pe.wait_ge(S["ctx"][fp], (j - fp) * 16 + 32)
                        project(1, w3, ctxT[:, fp, :, 0, :], S["kp"])

                    def project_v():
                        if m:
                            pe.wait_ge(S["pt_copied"], M * 4 + 3)
                        for bb in range(GB):
                            mm = pe.matmul(w0[:, bb * P:(bb + 1) * P], ctxT[:, fp, bb, :, :], wv[:], start=True, stop=True)
                        mm.then_inc(S["vp"], 1)

                    def back_attn():
                        pe.wait_ge(S["o_done"], B * 4 + 4)
                        for bb in range(GB):
                            mm = pe.matmul(w2[:, bb * SEQ:(bb + 1) * SEQ], on[:, par, bb, :], cst[:, C_ID2:C_ID2 + 64],
                                           start=True, stop=True)
                        mm.then_inc(S["at"], 1)

                    def back_out():
                        pe.wait_ge(S["at_copied"], B + 1)
                        pe.wait_ge(S["pt_copied"], B * 4 + 4)
                        for t in range(2):
                            mm = pe.matmul(w1[:, t * P:(t + 1) * P], aT[:, t * P:(t + 1) * P], wo[:], start=True, stop=True)
                        mm.then_inc(S["y"], 1)

                    def back_turn():
                        pe.wait_ge(S["xn2"], B + 1)
                        if f:
                            pe.wait_ge(S["q_read"], j + 1)
                        for t in range(2):
                            mm = pe.transpose(w2[:, t * P:(t + 1) * P], xn2[:, t, :], ident)
                        mm.then_inc(S["x2t"], 1)

                    def back_logits():
                        pe.wait_ge(S["x2t_copied"], B + 1)
                        if m:
                            pe.wait_ge(S["pt_copied"], M * 4 + 2)
                        E = (E0, E1)[L]
                        for t in range(2):
                            mm = pe.matmul(w1[:, t * E:(t + 1) * E], ysb[:, t * P:(t + 1) * P], wr[:, 0:E], start=True, stop=True)
                        mm.then_inc(S["lg"], 1)

                    def back_weights():
                        E = (E0, E1)[L]
                        pe.wait_ge(S["route_v"], R + 1)
                        if b:
                            if m:
                                pe.wait_ge(S["o_done"], M * 4 - 1)
                            else:
                                pe.wait_ge(S["o_done"], GROUPS * 4)
                        for t in range(2):
                            mm = pe.transpose(w3[0:2 * E, t * P:(t + 1) * P], rw[:, t * 2 * E:(t + 1) * 2 * E], ident)
                        mm.then_inc(S["rt"], 1)

                    if m: scores(0); scores(1)
                    if b: back_attn()
                    if f: turn_x()
                    if m: shift(0); scores(2); shift(1)
                    if b: back_out()
                    if r: back_weights()
                    if m: turn(0); scores(3); shift(2)
                    if f: project_q()
                    if m: turn(1); values(0); shift(3)
                    if b: back_turn()
                    if f: project_k()
                    if m: turn(2); values(1)
                    if b: back_logits()
                    if f: project_v()
                    if m: turn(3); values(2); values(3)

                slots(pe, step)

            def mixture(L):
                S = layers[L]
                chunks = (46, 32)[L]
                routed = (44, 32)[L]
                pe.wait_ge(s_ffw, (4 * 16, 9 * 16)[L])
                pe.wait_ge(s_sel, 16 * (L + 1))
                pe.wait_ge(S["x2_kept"], GROUPS)
                pe.wait_ge(S["rt_copied"], GROUPS)
                pe.wait_ge(S["x2t_copied"], GROUPS)
                pe.wait_ge(S["o_done"], GROUPS * 4)
                with pe.Fori(0, FGROUPS) as g:
                    k0 = g * chunks
                    toks = bass.ds(g * FTOK, FTOK)

                    def at(c):
                        return c * P if c <= routed else routed * P + (c - routed) * (SHARED // 2)

                    def down(c):
                        rows = SHARED // 2 if (L == 0 and c >= routed) else P
                        pe.wait_ge(S["hid"], k0 + (c + 1))
                        pe.matmul(bank[6][:, :], wdn[0:rows, c * P:(c + 1) * P], work2[0:rows, c % 3, :],
                                  start=(c == 0), stop=(c == chunks - 1 and L == 0), skip_group_check=True).then_inc(S["down"], 1)

                    for c in range(chunks):
                        rows = SHARED // 2 if (L == 0 and c >= routed) else P
                        if c >= 2:
                            pe.wait_ge(S["act"], k0 + (c - 1))
                            if L == 1:
                                pe.wait_ge(S["hid"], k0 + (c - 1))
                        pe.matmul(bank[c % 2][0:rows, :], wup[:, at(c):at(c) + rows], xn2T[:, toks],
                                  start=True, stop=True).then_inc(S["gate"], 1)
                        if L == 0:
                            if c >= 2:
                                pe.wait_ge(S["prod"], k0 + (c - 1))
                            pe.matmul(bank[2 + c % 2][0:rows, :], wup[:, ROWS0 + at(c):ROWS0 + at(c) + rows], xn2T[:, toks],
                                      start=True, stop=True).then_inc(S["up"], 1)
                        if c < routed:
                            if c >= 2 and L == 0:
                                pe.wait_ge(S["hid"], k0 + (c - 1))
                            lhsT = sel[:, c * P:(c + 1) * P] if L == 0 else sel1[:, (c // 4) * P:(c // 4 + 1) * P]
                            pe.matmul(bank[4 + c % 2][:, :], lhsT, rwT[0:lhsT.shape[0], toks],
                                      start=True, stop=True).then_inc(S["spread"], 1)
                        if c >= 2:
                            down(c - 2)
                    down(chunks - 2)
                    down(chunks - 1)
                    if L:
                        pe.matmul(bank[6][:, :], b2[:], rwT[0:2 * E1, toks].bitcast(F32), start=False, stop=True,
                                  skip_group_check=True).then_inc(S["down"], 1)
                    pe.wait_ge(S["y_copied"], g + 1)
                    for t in range(4):
                        mm = pe.transpose(bank[7][:, t * P:(t + 1) * P], ysb[:, t * P:(t + 1) * P], cst[:, C_ID:C_ID + P])
                    mm.then_inc(S["yt"], 1)
                    pe.wait_ge(S["x_done"], g + 1)

            for L in range(2):
                attention(L)
                mixture(L)

        @block.scalar
        def _(act):
            for L in range(2):
                S = layers[L]
                E = (E0, E1)[L]
                act.wait_ge(S["weights"], N_SMALL[L])
                act.activation(gates[:], gates[:], ACT.Tanh).then_inc(S["tanh"], 1)

                def load_ctx(j, par):
                    src = A["ctxT"][:, bass.ds(j * GTOK, GTOK)].rearrange("d (b s) -> d b s", s=SEQ)
                    for u in range(2):
                        act.dma_start(ctxT[:, par, :, u, :], src).then_inc(S["ctx"][par], 16)

                scale = (HD ** 0.5, HD ** -0.5)[L]

                def step(j, par, f, m, b, r):
                    M, B, R = j - 1, j - 2, j - 3

                    def copy_turned(u):
                        act.wait_ge(S["pt"], M * 4 + (u + 1))
                        act.activation(work2[:, u % 2, :], (w0, w1)[u % 2][:, :], ACT.Copy).then_inc(S["pt_copied"], 1)

                    def exps(u):
                        act.wait_ge(S["shifted"], M * 4 + (u + 1))
                        act.activation(work[:, u, :], score[u][:, :], ACT.Exp, scale=scale).then_inc(S["probs"], 1)

                    if first(j, 0):
                        load_ctx(0, 0)
                    if f and not first(j, GROUPS - 1):
                        if not first(j, 0):
                            act.wait_ge(S["vp"], j)
                        load_ctx(j + 1, 1 - par)
                    if b:
                        act.wait_ge(S["at"], B + 1)
                        act.activation(aT[:], w2[:, 0:GTOK], ACT.Copy).then_inc(S["at_copied"], 1)
                    if f:
                        act.wait_ge(S["xt"], j + 1)
                        act.activation(xnT[:, par, :], w0[:, 0:GTOK], ACT.Copy).then_inc(S["xt_copied"], 1)
                    if m:
                        exps(0)
                        exps(1)
                    if r:
                        act.wait_ge(S["rt"], R + 1)
                        act.activation(rwT[0:2 * E, bass.ds(R * GTOK, GTOK)], w3[0:2 * E, 0:GTOK], ACT.Copy).then_inc(S["rt_copied"], 1)
                    if m:
                        copy_turned(0)
                        exps(2)
                    if m:
                        copy_turned(1)
                        exps(3)
                    if f and L == 1:
                        act.wait_ge(S["qp"], j + 1)
                        if first(j, 0):
                            act.wait_ge(S["prep"], 1)
                        for h in range(4):
                            a = act.activation(qm[:, par, :, h, :], w2[:, 0:GTOK].rearrange("p (b s) -> p b s", s=SEQ), ACT.Identity,
                                               bias=bq4[:, h:h + 1], scale=cst[:, C_HM + h:C_HM + h + 1])
                        a.then_inc(S["q_masked"], 1)
                    if b:
                        act.wait_ge(S["x2t"], B + 1)
                        act.activation(ysb[:, 0:GTOK], w2[:, 0:GTOK], ACT.Copy).then_inc(S["x2t_copied"], 1)
                    if f and L == 0:
                        act.wait_ge(S["q_roped"], j + 1)
                        for h in range(4):
                            a = act.activation(qm[:, par, :, h, :], qr[:].rearrange("p (b s) -> p b s", s=SEQ), ACT.Copy,
                                               scale=cst[:, C_HM + h:C_HM + h + 1])
                        a.then_inc(S["q_masked"], 1)
                    if m:
                        copy_turned(2)
                    if b:
                        act.wait_ge(S["lg"], B + 1)
                        if L == 0:
                            act.activation(sg[:], w1[:, 0:2 * E0], ACT.Exp, scale=-1.0).then_inc(S["lg_read"], 1)
                        else:
                            act.activation(sg[:, 0:2 * E1], w1[:, 0:2 * E1], ACT.Copy).then_inc(S["lg_read"], 1)
                        act.wait_ge(S["x2t_copied"], B + 1)
                        act.activation(xn2T[:, bass.ds(B * GTOK, GTOK)], ysb[:, 0:GTOK], ACT.Copy).then_inc(S["x2_kept"], 1)
                        if L == 1:
                            act.wait_ge(S["v2a"], B + 1)
                            act.activation(sc[:, 0:2 * E1], choice[:, 0:2 * E1], ACT.Exp).then_inc(S["a2v"], 1)
                    if m:
                        copy_turned(3)

                slots(act, step)

                chunks = (46, 32)[L]
                routed = (44, 32)[L]
                with act.Fori(0, FGROUPS) as g:
                    for c in range(chunks):
                        rows = SHARED // 2 if (L == 0 and c >= routed) else P
                        act.wait_ge(S["gate"], g * chunks + (c + 1))
                        if c >= 2:
                            act.wait_ge(S["hid"] if L else S["prod"], g * chunks + (c - 1))
                        if L == 0:
                            act.activation(work[0:rows, c % 2, :], bank[c % 2][0:rows, :], ACT.Silu).then_inc(S["act"], 1)
                        else:
                            act.activation(work[:, c % 2, :], bank[c % 2][:, :], ACT.Gelu_apprx_tanh,
                                           bias=b1[:, c:c + 1]).then_inc(S["act"], 1)
                    act.wait_ge(S["down"], (g + 1) * (chunks + L))
                    act.activation(ysb[:], bank[6][:, :], ACT.Copy).then_inc(S["y_copied"], 1)

        @block.vector
        def _(dve):
            dve.wait_ge(s_const, 16)
            dve.tensor_copy(idr[:], cst[:, C_ID:C_ID + P]).then_inc(s_setup, 1)
            dve.tensor_copy(idb[:], cst[:, C_ID:C_ID + P]).then_inc(s_setup, 1)
            dve.tensor_copy(band[:], cst[:, C_BAND:C_BAND + 64]).then_inc(s_setup, 1)
            dve.wait_ge(s_x, 64)
            dve.tensor_copy(vm[:, :, :, :, 32:34].rearrange("p a b s c -> p (a b s) c"),
                            cst[:, C_JM:C_JM + 2].unsqueeze(1).to_broadcast([P, 2 * GB * STRIPS, 2])).then_inc(s_ones, 1)

            for L in range(2):
                S = layers[L]
                E = (E0, E1)[L]
                dve.wait_ge(S["tanh"], 1)
                dve.tensor_scalar(gbo[:], brow[:, 0, :], gates[:, L:L + 1], None, ALU.mult)
                if L:
                    dve.tensor_tensor(bvm[:].rearrange("p (s c) -> p s c", c=32), brow[:, 1, :].rearrange("p (s c) -> p s c", c=32),
                                      cst[:, C_VM:C_VM + 32].unsqueeze(1).to_broadcast([P, 4, 32]), ALU.mult)
                dve.tensor_scalar(bq4[:], cst[:, C_HM:C_HM + 4], bcol[:, 0:1] if L else 0.0, None, ALU.mult).then_inc(S["prep"], 1)

                def step(j, par, f, m, b, r):
                    M, B, R = j - 1, j - 2, j - 3
                    mp = 1 - par

                    def norm_stats():
                        for t in range(2):
                            a = dve.bn_stats(st[:, par, t, :], x[:, bass.ds(j * GTOK + t * P, P)])
                        a.then_inc(S["stats"], 1)
                        hold(dve, S["stats"], j + 1)
                        for t in range(2):
                            a = dve.bn_aggr(mv[:, par, t, :], st[:, par, t, :])
                        a.then_inc(S["varp"], 1)

                    def norm_apply():
                        dve.wait_ge(S["rstd"], j * 2 + 2)
                        for t in range(2):
                            a = dve.tensor_scalar(xn[:, par, t, :], x[:, bass.ds(j * GTOK + t * P, P)],
                                                  mv[:, par, t, 0:1], rs[:, par, t:t + 1], ALU.subtract, ALU.mult)
                        a.then_inc(S["xn"], 1)

                    def max_rows(u):
                        dve.wait_ge(S["scores"], M * 4 + (u + 1))
                        dve.tensor_reduce(nmax[:, u, :], score[u][:].rearrange("p (a k) -> p a k", k=SEQ), AX.X, ALU.max,
                                          negate=True).then_inc(S["max_done"], 1)

                    def outs(u):
                        w = (w3, w2)[u % 2]
                        dve.wait_ge(S["op"], M * 4 + (u + 1))
                        o = w[:, 0:GB * VW].rearrange("p (b c) -> p b c", c=VW)
                        dve.reciprocal(rden[:, mp, :, :], o[:, :, 32:34]).then_inc(S["rden"], 1)
                        dve.wait_ge(S["rden"], M * 4 + (u + 1))
                        dve.tensor_tensor(rdm[:, mp, :, :, :], rden[:, mp, :, :].unsqueeze(3).to_broadcast([P, GB, 2, 2]),
                                          cst[:, C_JM:C_JM + 2].unsqueeze(1).unsqueeze(1).to_broadcast([P, GB, 2, 2]),
                                          ALU.mult).then_inc(S["rdm"], 1)
                        dve.wait_ge(S["rdm"], M * 4 + (u + 1))
                        dve.tensor_tensor(on[:, mp, :, 32 * u:32 * u + 32].rearrange("p b (h d) -> p b h d", d=HD),
                                          o[:, :, 0:32].rearrange("p b (h d) -> p b h d", d=HD),
                                          rdm[:, mp, :, :, :].rearrange("p b q r -> p b (q r)").unsqueeze(3).to_broadcast([P, GB, 4, HD]),
                                          ALU.mult).then_inc(S["o_done"], 1)

                    def rotate(n, w, ready, read):
                        dve.wait_ge(ready, j + 1)
                        if n == 0:
                            if not first(j, 0):
                                dve.wait_ge(S["q_roped"], j)
                        else:
                            if not first(j, 0):
                                dve.wait_ge(S["k_done"], j)
                        for h in range(2):
                            a = dve.tensor_tensor(rope[:, 2 * n + h, :].rearrange("p (b s) -> p b s", s=SEQ),
                                                  w[:, h * GTOK:(h + 1) * GTOK].rearrange("p (b s) -> p b s", s=SEQ),
                                                  cst[:, C_COS + 64 * h:C_COS + 64 * h + 64].unsqueeze(1).to_broadcast([P, GB, 64]),
                                                  ALU.mult)
                        a.then_inc(read, 1)

                    def mask_values():
                        dve.wait_ge(S["vp"], j + 1)
                        dve.tensor_tensor(vm[:, par, :, :, 0:32],
                                          w0[:].rearrange("p (b s c) -> p b s c", b=GB, c=32),
                                          cst[:, C_VM:C_VM + 32].unsqueeze(1).unsqueeze(1).to_broadcast([P, GB, 4, 32]),
                                          ALU.mult).then_inc(S["v_masked"], 1)

                    def residual():
                        dve.wait_ge(S["y"], B + 1)
                        dve.wait_ge(S["xb"], B + 1)
                        xs = x[:, bass.ds(B * GTOK, GTOK)]
                        dve.scalar_tensor_tensor(xs, w1[:, 0:GTOK], gates[:, L:L + 1], xb[:, par, :], ALU.mult, ALU.add).then_inc(S["resid"], 1)
                        hold(dve, S["resid"], B + 1)
                        for t in range(2):
                            a = dve.bn_stats(st2[:, t, :], x[:, bass.ds(B * GTOK + t * P, P)])
                        a.then_inc(S["stats2"], 1)
                        hold(dve, S["stats2"], B + 1)
                        for t in range(2):
                            a = dve.bn_aggr(mv2[:, t, :], st2[:, t, :])
                        a.then_inc(S["varp2"], 1)

                    def norm2_apply():
                        dve.wait_ge(S["rstd2"], B * 2 + 2)
                        for t in range(2):
                            a = dve.tensor_scalar(xn2[:, t, :], x[:, bass.ds(B * GTOK + t * P, P)],
                                                  mv2[:, t, 0:1], rs2[:, t:t + 1], ALU.subtract, ALU.mult)
                        a.then_inc(S["xn2"], 1)

                    def route_scores():
                        dve.wait_ge(S["lg_read"], B + 1)
                        dve.tensor_scalar(sc[:], sg[:], 1.0, None, ALU.add).then_inc(S["v2a"], 1)
                        dve.wait_ge(S["v2a"], B * 3 + 1)
                        dve.reciprocal(sc[:], sc[:]).then_inc(S["v2a"], 1)
                        dve.wait_ge(S["v2a"], B * 3 + 2)
                        dve.tensor_tensor(choice[:].rearrange("p (t e) -> p t e", e=E0), sc[:].rearrange("p (t e) -> p t e", e=E0),
                                          brow[:, 1, 0:E0].unsqueeze(1).to_broadcast([P, 2, E0]), ALU.add).then_inc(S["v2a"], 1)
                        hold(dve, S["v2a"], B * 3 + 3)
                        for g in range(16):
                            a = dve.max(gtop[:, g, :], choice[:, g * 8:(g + 1) * 8])
                        a.then_inc(S["v2p"], 1)

                    def route_logits():
                        lg = sg[:, 0:2 * E1].rearrange("p (t e) -> p t e", e=E1)
                        dve.wait_ge(S["lg_read"], B + 1)
                        dve.tensor_reduce(top8[:, 0, 0:2], lg, AX.X, ALU.max).then_inc(S["v2p"], 1)
                        dve.wait_ge(S["v2p"], B + 1)
                        dve.tensor_tensor(choice[:, 0:2 * E1].rearrange("p (t e) -> p t e", e=E1), lg,
                                          top8[:, 0, 0:2].unsqueeze(2).to_broadcast([P, 2, E1]), ALU.subtract).then_inc(S["v2a"], 1)

                    def route_weights():
                        steps = (10, 5)[L]
                        n = [0]

                        def link(ins):
                            n[0] += 1
                            ins.then_inc(S["chain"], 1)
                            hold(dve, S["chain"], R * steps + n[0])
                        ws = wsel[:, 0:2 * E]
                        wt = ws.rearrange("p (t e) -> p t e", e=E)
                        parts = rw[:, 0:4 * E].rearrange("p (t a e) -> p t a e", t=2, a=2)
                        kept = rwr[:, 0:2 * E]
                        hold(dve, S["p2v"], R + 1)
                        if not first(R, 0):
                            hold(dve, S["rt"], R)
                        if L == 0:
                            for t in range(2):
                                ch = masked[:, t * E:(t + 1) * E]
                                link(dve.max(top8[:, t, :], ch))
                                link(dve.match_replace(rest[:, t * E:(t + 1) * E], top8[:, t, :], ch, MASKED))
                            link(dve.scalar_tensor_tensor(ws, rest[:], MASKED * 0.5, sc[:], ALU.is_lt, ALU.mult))
                        else:
                            dve.wait_ge(S["a2v"], R + 1)
                            link(dve.tensor_tensor(ws, sc[:, 0:2 * E], masked[:, 0:2 * E], ALU.mult))
                        link(dve.tensor_reduce(wsum[:], wt, AX.X, ALU.add))
                        if L == 0:
                            link(dve.tensor_scalar(wsum[:], wsum[:], 1e-20, None, ALU.add))
                        link(dve.reciprocal(wsum[:], wsum[:]))
                        link(dve.scalar_tensor_tensor(wt, wt, (RSCALE, 1.0)[L], wsum[:].unsqueeze(2).to_broadcast([P, 2, E]),
                                                      ALU.mult, ALU.mult))
                        link(dve.tensor_copy(kept, ws))
                        dve.tensor_copy(parts[:, :, 0, :], kept.bitcast(F32).rearrange("p (t e) -> p t e", e=E))
                        dve.tensor_tensor(parts[:, :, 1, :], wt, kept.bitcast(F32).rearrange("p (t e) -> p t e", e=E),
                                          ALU.subtract).then_inc(S["route_v"], 1)
                        assert n[0] == steps, n[0]

                    if f:
                        norm_stats()
                    if m:
                        max_rows(0)
                        max_rows(1)
                    if f:
                        norm_apply()
                    if m:
                        max_rows(2)
                    if b:
                        residual()
                    if r:
                        route_weights()
                    if m:
                        max_rows(3)
                    if f and L == 0:
                        rotate(0, w2, S["qp"], S["q_read"])
                    if b:
                        norm2_apply()
                    if m:
                        outs(0)
                    if f:
                        if L == 0:
                            rotate(1, w3, S["kp"], S["k_read"])
                        else:
                            dve.wait_ge(S["kp"], j + 1)
                            dve.tensor_scalar(kr[:, par, :], w3[:, 0:GTOK], bcol[:, 1:2], None, ALU.add).then_inc(S["k_done"], 1)
                    if m:
                        outs(1)
                    if f:
                        mask_values()
                    if b:
                        if L == 0:
                            route_scores()
                        else:
                            route_logits()
                    if m:
                        outs(2)
                        outs(3)

                slots(dve, step)

                chunks = (46, 32)[L]
                routed = (44, 32)[L]
                dve.wait_ge(S["pt_copied"], GROUPS * 4)
                with dve.Fori(0, FGROUPS) as g:
                    k0 = g * chunks

                    def weigh(c):
                        if L == 0:
                            dve.wait_ge(S["prod"], k0 + (c + 1))
                        else:
                            dve.wait_ge(S["act"], k0 + (c + 1))
                        dve.wait_ge(S["spread"], g * routed + (c + 1))
                        if c >= 3:
                            dve.wait_ge(S["down"], g * (chunks + L) + (c - 2))
                        src = work[:, 2 + c % 2, :] if L == 0 else work[:, c % 2, :]
                        dve.tensor_tensor(work2[:, c % 3, :], src, bank[4 + c % 2][:, :], ALU.mult).then_inc(S["hid"], 1)

                    for c in range(chunks):
                        if L == 0:
                            rows = SHARED // 2 if c >= routed else P
                            dve.wait_ge(S["act"], k0 + (c + 1))
                            dve.wait_ge(S["up"], k0 + (c + 1))
                            dve.tensor_tensor(work[0:rows, 2 + c % 2, :], work[0:rows, c % 2, :], bank[2 + c % 2][0:rows, :],
                                              ALU.mult).then_inc(S["prod"], 1)
                            if c >= routed:
                                dve.wait_ge(S["prod"], k0 + (c + 1))
                                dve.wait_ge(S["down"], k0 + (c - 2))
                                dve.tensor_copy(work2[0:rows, c % 3, :], work[0:rows, 2 + c % 2, :]).then_inc(S["hid"], 1)
                                continue
                        weigh(c)
                    dve.wait_ge(S["yt"], g + 1)
                    xs = x[:, bass.ds(g * FTOK, FTOK)]
                    dve.scalar_tensor_tensor(xs, bank[7][:, :], gates[:, 2 + L:3 + L], xs, ALU.mult, ALU.add).then_inc(S["x_done"], 1)
                dve.wait_ge(S["x_done"], FGROUPS)

        @block.gpsimd
        def _(pool):
            pool.memset(mhalf[:], -0.5).then_inc(s_half, 1)
            pool.dma_start(sel[:], A["sel0"]).then_inc(s_sel, 16)
            pool.wait_ge(s_half, 1)
            for L in range(2):
                S = layers[L]
                pool.wait_ge(S["prep"], 1)
                if L:
                    pool.dma_start(sel1, A["sel1"]).then_inc(s_sel, 16)

                def step(j, par, f, m, b, r):
                    M, B, R = j - 1, j - 2, j - 3
                    if b:
                        if not first(B, 0):
                            pool.wait_ge(S["resid"], B)
                        pool.tensor_tensor(xb[:, par, :].rearrange("p (t d) -> p t d", d=P),
                                           x[:, bass.ds(B * GTOK, GTOK)].rearrange("p (t d) -> p t d", d=P),
                                           gbo[:].unsqueeze(1).to_broadcast([P, 2, P]), ALU.add).then_inc(S["xb"], 1)
                    if f:
                        hold(pool, S["varp"], j + 1)
                        pool.tensor_scalar(ve[:, par, :], mv[:, par, :, 1], EPS, None, ALU.add).then_inc(S["rstd"], 1)
                        pool.wait_ge(S["rstd"], j * 2 + 1)
                        pool.tensor_tensor(rs[:, par, :], ve[:, par, :], mhalf[:], ALU.pow).then_inc(S["rstd"], 1)
                    if b:
                        hold(pool, S["varp2"], B + 1)
                        pool.tensor_scalar(ve2[:], mv2[:, :, 1], EPS, None, ALU.add).then_inc(S["rstd2"], 1)
                        pool.wait_ge(S["rstd2"], B * 2 + 1)
                        pool.tensor_tensor(rs2[:], ve2[:], mhalf[:], ALU.pow).then_inc(S["rstd2"], 1)
                    if f and L == 0:
                        pool.wait_ge(S["q_read"], j + 1)
                        if not first(j, 0):
                            pool.wait_ge(S["q_masked"], j)
                        pool.tensor_tensor(qr[:], rope[:, 0, :], rope[:, 1, :], ALU.add).then_inc(S["q_roped"], 1)
                        pool.wait_ge(S["k_read"], j + 1)
                        pool.tensor_tensor(kr[:, par, :], rope[:, 2, :], rope[:, 3, :], ALU.add).then_inc(S["k_done"], 1)
                    if f and L == 1:
                        pool.wait_ge(S["v_masked"], j + 1)
                        v = vm[:, par, :, :, 0:32]
                        pool.tensor_tensor(v, v, bvm[:].rearrange("p (s c) -> p s c", c=32).unsqueeze(1).to_broadcast([P, GB, 4, 32]),
                                           ALU.add).then_inc(S["v_done"], 1)
                    if b and L == 0:
                        pool.wait_ge(S["v2p"], B + 1)
                        route0(B)
                    if b and L == 1:
                        pool.wait_ge(S["lg_read"], B + 1)
                        route1(B)

                def ranks(link, val):
                    for t in range(2):
                        vj = val[:, t * 8:t * 8 + 8].unsqueeze(1).to_broadcast([P, 8, 8])
                        vi = val[:, t * 8:t * 8 + 8].unsqueeze(2).to_broadcast([P, 8, 8])
                        gt = cmp[:, 0, t * 64:t * 64 + 64].rearrange("p (i j) -> p i j", j=8)
                        eq = cmp[:, 1, t * 64:t * 64 + 64].rearrange("p (i j) -> p i j", j=8)
                        link(pool.tensor_tensor(gt, vj, vi, ALU.subtract))
                        link(pool.tensor_scalar(eq, gt, 0.0, None, ALU.is_equal))
                        link(pool.tensor_scalar(gt, gt, 0.0, None, ALU.is_gt))
                        link(pool.tensor_tensor(eq, eq, cst[:, C_TRI:C_END].rearrange("p (i j) -> p i j", j=8), ALU.mult))
                    link(pool.tensor_tensor(cmp[:, 0, :], cmp[:, 0, :], cmp[:, 1, :], ALU.add))
                    c = cmp[:, 0, :].rearrange("p (i j) -> p i j", j=8)
                    link(pool.tensor_tensor(cmp[:, 1, 0:64].rearrange("p (i j) -> p i j", j=4), c[:, :, 0:4], c[:, :, 4:8], ALU.add))
                    c = cmp[:, 1, 0:64].rearrange("p (i j) -> p i j", j=4)
                    link(pool.tensor_tensor(cmp[:, 0, 0:32].rearrange("p (i j) -> p i j", j=2), c[:, :, 0:2], c[:, :, 2:4], ALU.add))
                    c = cmp[:, 0, 0:32].rearrange("p (i j) -> p i j", j=2)
                    link(pool.tensor_tensor(rank[:], c[:, :, 0], c[:, :, 1], ALU.add))

                def route0(B):
                    n = [0]

                    def link(ins):
                        n[0] += 1
                        ins.then_inc(S["route_p"], 1)
                        hold(pool, S["route_p"], B * 14 + n[0])
                    link(pool.tensor_tensor(gsum[:], gtop[:, :, 0], gtop[:, :, 1], ALU.add))
                    ranks(link, gsum)
                    link(pool.tensor_scalar(rank[:], rank[:], float(TOPG0), None, ALU.is_lt))
                    if not first(B, 0):
                        pool.wait_ge(S["route_v"], B)
                    pool.tensor_tensor(masked[:].rearrange("p (g e) -> p g e", e=8), choice[:].rearrange("p (g e) -> p g e", e=8),
                                       rank[:].unsqueeze(2).to_broadcast([P, 16, 8]), ALU.mult).then_inc(S["p2v"], 1)
                    assert n[0] == 14, n[0]

                def route1(B):
                    n = [0]

                    def link(ins):
                        n[0] += 1
                        ins.then_inc(S["route_p"], 1)
                        hold(pool, S["route_p"], B * 12 + n[0])
                    ranks(link, sg)
                    if not first(B, 0):
                        hold(pool, S["route_v"], B)
                    pool.tensor_scalar(masked[:, 0:16], rank[:], 2.0, None, ALU.is_lt).then_inc(S["p2v"], 1)
                    assert n[0] == 12, n[0]

                slots(pool, step)


def kernel(**inputs):
    import concourse.bacc as _bacc
    from concourse.bass_utils import run_bass_kernel_spmd as _run

    I = {k: np.asarray(v) for k, v in inputs.items()}
    swap = np.concatenate([np.arange(64, 128), np.arange(0, 64)])
    a = {"cst": constants(), "sel0": spread_rows(E0, I0, ROUTED0), "x": I["x"]}
    a["sel1"] = np.repeat(np.concatenate([np.eye(E1, dtype=np.float32)] * 2)[:, :, None], P, axis=2).reshape(2 * E1, E1 * P)
    a["ctxT"] = I["ctx_1024"].reshape(TOK, D).T
    for n in ("g_xattn", "g_ffn", "L0_ffn_gate_bias", "L1_ffn_b2"):
        a[n] = I[n]
    for s in "qk":
        w = I["L0_xattn_w" + s].T
        a["L0_w" + s] = np.concatenate([w, w[:, swap]], axis=1)
        a["L1_w" + s] = I["L1_xattn_W_" + s]
    a["L0_wv"], a["L1_wv"] = I["L0_xattn_wv"].T, I["L1_xattn_W_v"]
    a["L0_wo"], a["L1_wo"] = I["L0_xattn_wo_w"].T, I["L1_xattn_W_o"]
    a["L0_bo"], a["L1_bo"] = I["L0_xattn_wo_b"], I["L1_xattn_b_o"]
    a["L1_bq"], a["L1_bk"], a["L1_bv"] = I["L1_xattn_b_q"], I["L1_xattn_b_k"], I["L1_xattn_b_v"]
    a["L0_router"], a["L1_router"] = I["L0_ffn_gate_w"].T, I["L1_ffn_Wg"]
    a["gate0"] = np.concatenate([I["L0_ffn_Wg"].reshape(ROUTED0, D), I["L0_ffn_Sg"]]).T
    a["up0"] = np.concatenate([I["L0_ffn_Wu"].reshape(ROUTED0, D), I["L0_ffn_Su"]]).T
    a["down0"] = np.concatenate([I["L0_ffn_Wd"].transpose(0, 2, 1).reshape(ROUTED0, D), I["L0_ffn_Sd"].T])
    a["w1"] = I["L1_ffn_W1"].transpose(1, 0, 2).reshape(D, ROWS1)
    a["w2"] = I["L1_ffn_W2"].reshape(ROWS1, D)
    a["b1"] = I["L1_ffn_b1"].reshape(ROWS1 // P, P).T

    nc = _bacc.Bacc("TRN2", target_bir_lowering=False, num_devices=1)
    arrays, args = {}, {}
    for name, v in a.items():
        v = np.ascontiguousarray(v)
        arrays[f"in_{name}"] = v
        args[name] = nc.dram_tensor(f"in_{name}", v.shape, mybir.dt.from_np(v.dtype), kind="ExternalInput").ap()
    out = nc.dram_tensor("out_0", (BATCH, SEQ, D), F32, kind="ExternalOutput").ap()
    build(nc, args, out)
    r = _run(nc, [arrays], core_ids=[0])
    return r.results[0]["out_0"]
```

```python
import numpy as np
from contextlib import ExitStack

import concourse.bass as bass
from concourse import mybir

ALU = mybir.AluOpType
ACT = mybir.ActivationFunctionType
AX = mybir.AxisListType
F32 = mybir.dt.float32
F32R = mybir.dt.float32r
BF16 = mybir.dt.bfloat16

P = 128
BATCH, SEQ, D = 64, 64, 128
TOK = BATCH * SEQ
HEADS, HD = 16, 8
EPS = 1e-5
MASKED = -1e30

GB = 4
GTOK = GB * SEQ
GROUPS = TOK // GTOK
LAGS = 8
STRIPS = 4
VW = 34

E0, I0, TOPG0 = 64, 88, 4
SHARED = 176
RSCALE = 2.5
ROUTED0 = E0 * I0
STRIP_E = 16
E1, F1 = 8, 512
ROUTED = (ROUTED0 // P, E1 * F1 // P)
CHUNKS = (ROUTED[0] + -(-SHARED // P), ROUTED[1])
CW = (3 * P, 2 * P)
RING = (4, 8)
AHEAD = (1, 4)
DLAG = (2, 3)
FTOK = 512
FGROUPS = TOK // FTOK

C_ID, C_ID2, C_VM, C_JM, C_HM, C_COS, C_SIN, C_BAND, C_TRI, C_END = (
    0, 128, 192, 224, 226, 230, 294, 358, 422, 486)


def constants():
    c = np.zeros((P, C_END), np.float32)
    row = np.arange(P)
    c[:, C_ID:C_ID2] = np.eye(P)
    c[:, C_ID2:C_VM] = (row % 64)[:, None] == np.arange(64)
    c[:, C_VM:C_JM] = (row // 64)[:, None] == (np.arange(32) // 16)
    c[:, C_JM:C_HM] = (row // 64)[:, None] == np.arange(2)
    c[:, C_HM:C_COS] = ((row % 32) // HD)[:, None] == np.arange(4)
    half = D // 2
    inv = np.float32(1.0) / np.float32(10000.0) ** (np.arange(half, dtype=np.float32) / np.float32(half))
    ang = np.arange(SEQ, dtype=np.float32)[:, None] * inv[None, :]
    cos, sin = np.cos(ang).T, np.sin(ang).T
    c[:, C_COS:C_SIN] = np.concatenate([cos, cos])
    c[:half, C_SIN:C_BAND] -= sin
    c[half:, C_SIN:C_BAND] += sin
    q, k = (row % 64)[:, None], np.arange(64)[None, :]
    c[:, C_BAND:C_TRI] = np.where(abs(q - k) <= 32, 0.0, MASKED)
    i, j = np.arange(8)[:, None], np.arange(8)[None, :]
    c[:, C_TRI:C_END] = (j < i).reshape(1, 64)
    return c


def spread_rows():
    row = np.arange(P)
    sel0 = (row % STRIP_E)[:, None] == (np.arange(STRIP_E * I0) // I0)[None, :]
    sel1 = (np.arange(2 * E1) % E1)[:, None] == (np.arange(E1 * P) // P)[None, :]
    return sel0.astype(np.float32), sel1.astype(np.float32)


def build(nc, A, out):
    x_dram = A["x"].rearrange("b s d -> (b s) d").rearrange("(t p) d -> p t d", p=P)
    out_dram = out.rearrange("b s d -> (b s) d").rearrange("(t p) d -> p t d", p=P)

    with ExitStack() as ctx:
        def sb(name, shape, dt=F32):
            return ctx.enter_context(nc.sbuf_tensor(name, shape, dt))

        def sem(name):
            return ctx.enter_context(nc.semaphore(name))

        bank = [ctx.enter_context(nc.psum_tensor(f"bank{i}", [P, 512], F32)) for i in range(8)]
        score = bank[0:4]
        w0, w1, w2, w3 = bank[4:8]

        x = sb("x", [P, TOK])
        xn2T = sb("xn2T", [P, TOK])
        rwT = sb("rwT", [P, TOK], F32R)
        cst = sb("cst", [P, C_END])
        idr = sb("idr", [P, P], F32R)
        band = sb("band", [P, 64], BF16)
        idb = sb("idb", [P, P], BF16)
        weights = sb("weights", [P, CHUNKS[0] * CW[0]])
        sel = sb("sel", [P, STRIP_E * I0], F32R)
        sel1 = sel[0:2 * E1, 0:E1 * P]
        gates = sb("gates", [P, 4])
        mhalf = sb("mhalf", [P, 2])
        idle = sb("idle", [P, 48])

        wq = sb("wq", [P, 2, 2 * P])
        wv = sb("wv", [P, P])
        wo = sb("wo", [P, P])
        wr = sb("wr", [P, E0])
        brow = sb("brow", [P, 3, P])
        bcol = sb("bcol", [P, 2])
        bq4 = sb("bq4", [P, 4])
        b1 = sb("b1", [P, 32])
        b2 = sb("b2", [2 * E1, P])
        gbo = sb("gbo", [P, P])
        bvm = sb("bvm", [P, P])

        with nc.sbuf_tensor("arena", [P, 6144], F32) as arena:
            pass
        ctxT = arena[:, 0:1024].rearrange("p (u b c s) -> p u b c s", u=2, b=GB, c=2)
        wring = sb("wring", [P, RING[1] * 2 * CW[1]], F32R)
        hsplit = sb("hsplit", [P, 2, 2, FTOK], F32R)
        wsplits = [wring[:, 0:RING[L] * 2 * CW[L]].rearrange("p (r a n) -> p r a n", r=RING[L], a=2) for L in range(2)]
        st = sb("st", [P, 2, 2, 6])
        mv = sb("mv", [P, 2, 2, 2])
        ve = sb("ve", [P, 2, 2])
        rs = sb("rs", [P, 2, 2])
        xn = sb("xn", [P, 2, 2, P])
        xnT = arena[:, 1024:1536].rearrange("p (u n) -> p u n", u=2)
        rope = arena[:, 1536:2560].rearrange("p (u n) -> p u n", u=4)
        qr = sb("qr", [P, GTOK])
        qm = arena[:, 2560:4608].rearrange("p (u b h s) -> p u b h s", u=2, b=GB, h=4)
        kr = arena[:, 4608:5120].rearrange("p (u n) -> p u n", u=2)
        vm = sb("vm", [P, 2, GB, STRIPS, VW])
        nmax = sb("nmax", [P, 4, 8], F32R)
        work = sb("work", [P, 4, 512])
        work2 = sb("work2", [P, 2, 512])
        rden = sb("rden", [P, 2, GB, 2])
        rdm = sb("rdm", [P, 2, GB, 2, 2])
        on = arena[:, 5120:6144].rearrange("p (u b e) -> p u b e", u=2, b=GB)
        aT = sb("aT", [P, GTOK])
        xb = sb("xb", [P, 2, GTOK])
        st2 = sb("st2", [P, 2, 6])
        mv2 = sb("mv2", [P, 2, 2, 2])
        ve2 = sb("ve2", [P, 2, 2])
        rs2 = sb("rs2", [P, 2, 2])
        xn2 = sb("xn2", [P, 2, P])
        ysb = sb("ysb", [P, FTOK])
        xin = sb("xin", [P, 2, 3, FTOK], F32R)
        sg = sb("sg", [P, 2 * E0])
        sc = sb("sc", [P, 2 * E0])
        choice = sb("choice", [P, 2 * E0])
        gtop = sb("gtop", [P, 16, 8])
        gsum = sb("gsum", [P, 16])
        cmp = sb("cmp", [P, 2, P])
        rank = sb("rank", [P, 16])
        masked = sb("masked", [P, 2 * E0])
        top8 = sb("top8", [P, 2, 8])
        rest = sb("rest", [P, 2 * E0])
        wsel = sb("wsel", [P, 2 * E0])
        wsum = sb("wsum", [P, 2])
        rw = sb("rw", [P, 4 * E0])
        rwr = sb("rwr", [P, 2 * E0], F32R)

        s_const = sem("s_const"); s_x = sem("s_x"); s_ffw = sem("s_ffw"); s_sel = sem("s_sel")
        s_setup = sem("s_setup"); s_half = sem("s_half"); s_ones = sem("s_ones")
        s_out = sem("s_out")

        def layer_semaphores(L):
            names = (
                "weights", "tanh", "prep",
                "stats", "varp", "rstd", "xn", "xt", "xt_copied", "qp", "q_read", "q_roped", "q_masked",
                "kp", "k_read", "k_done", "vp", "v_masked", "v_done",
                "scores", "max_done", "shifted", "probs", "pt", "pt_copied", "op", "rden", "rdm", "o_done",
                "at", "at_copied", "xb", "y", "resid", "stats2", "varp2", "rstd2", "xn2", "x2t", "x2t_copied",
                "x2_kept", "lg", "lg_read", "route_v", "route_p", "p2v", "v2p", "rt", "rt_copied", "a2v", "v2a", "chain",
                "x_hi", "x_lo", "w_hi", "w_lo", "gate", "up", "spread", "act", "prod", "hid", "h_hi", "h_lo", "down",
                "y_copied", "yt", "x_done")
            S = {name: sem(f"{name}{L}") for name in names}
            S["ctx"] = [sem(f"ctx_loaded{L}_{i}") for i in range(2)]
            if L == 1:
                S["q_read"], S["k_read"] = S["q_masked"], S["k_done"]
            return S

        layers = [layer_semaphores(0), layer_semaphores(1)]

        block = ctx.enter_context(nc.Block())

        def first(value, n):
            return isinstance(value, int) and value == n

        held = {}

        def hold(eng, semaphore, value):
            eng.wait_ge(semaphore, value)
            if not isinstance(value, int):
                n = held.setdefault((eng.engine, semaphore.name), len(held))
                if eng.engine == mybir.EngineType.Pool:
                    eng.tensor_tensor(idle[:, n:n + 1], mhalf[:, 0:1], mhalf[:, 1:2], ALU.add)
                else:
                    eng.tensor_copy(idle[:, n:n + 1], cst[:, 0:1])

        def slots(eng, step):
            def has_group(j):
                return [0 <= j - lag < GROUPS for lag in range(LAGS)]

            for j in range(LAGS):
                step(j, j % 2, *has_group(j))
            with eng.Fori(0, (GROUPS - LAGS) // 2) as i:
                for h in range(2):
                    step(i * 2 + LAGS + h, h, *has_group(LAGS))
            for j in range(GROUPS, GROUPS + LAGS - 1):
                step(j, j % 2, *has_group(j))

        def pairs(eng, group):
            group(0, 0)
            with eng.Fori(0, (FGROUPS - 2) // 2) as i:
                group(i * 2 + 1, 1)
                group(i * 2 + 2, 0)
            group(FGROUPS - 1, 1)

        @block.sync
        def _(sp):
            sp.dma_start(cst[:], A["cst"]).then_inc(s_const, 16)
            S = layers[0]

            def small(L, S):
                pre = f"L{L}_"
                sp.dma_start(gates[:, 0:2], A["g_xattn"].rearrange("(a n) -> a n", a=1).to_broadcast([P, 2])).then_inc(S["weights"], 16)
                sp.dma_start(gates[:, 2:4], A["g_ffn"].rearrange("(a n) -> a n", a=1).to_broadcast([P, 2])).then_inc(S["weights"], 16)
                for n, s in enumerate(("q", "k")):
                    src = A[pre + "w" + s]
                    sp.dma_start(wq[:, n, 0:src.shape[1]], src).then_inc(S["weights"], 16)
                sp.dma_start(wv[:], A[pre + "wv"]).then_inc(S["weights"], 16)
                sp.dma_start(wo[:], A[pre + "wo"]).then_inc(S["weights"], 16)
                r = A[pre + "router"]
                sp.dma_start(wr[:, 0:r.shape[1]], r).then_inc(S["weights"], 16)
                sp.dma_start(brow[:, 0, :], A[pre + "bo"].rearrange("(a n) -> a n", a=1).to_broadcast([P, P])).then_inc(S["weights"], 16)
                if L == 0:
                    sp.dma_start(brow[:, 1, 0:E0], A["L0_ffn_gate_bias"].rearrange("(a n) -> a n", a=1).to_broadcast([P, E0])).then_inc(S["weights"], 16)
                else:
                    sp.dma_start(brow[:, 1, :], A["L1_bv"].rearrange("(a n) -> a n", a=1).to_broadcast([P, P])).then_inc(S["weights"], 16)
                    sp.dma_start(bcol[:, 0:1], A["L1_bq"].rearrange("(n a) -> n a", a=1)).then_inc(S["weights"], 16)
                    sp.dma_start(bcol[:, 1:2], A["L1_bk"].rearrange("(n a) -> n a", a=1)).then_inc(S["weights"], 16)

            small(0, layers[0])
            for t in range(0, 32, 8):
                sp.dma_start(x[:, t * P:(t + 8) * P].rearrange("p (t d) -> p t d", d=P), x_dram[:, t:t + 8, :]).then_inc(s_x, 16)
            for part in range(2):
                cols = slice(part * CHUNKS[0] // 2 * CW[0], (part + 1) * CHUNKS[0] // 2 * CW[0])
                sp.dma_start(weights[:, cols], A["mix0"][:, cols]).then_inc(s_ffw, 16)
            sp.wait_ge(layers[0]["x_done"], FGROUPS)
            small(1, layers[1])
            sp.dma_start(weights[:, 0:CHUNKS[1] * CW[1]], A["mix1"]).then_inc(s_ffw, 16)
            sp.dma_start(b1[:], A["b1"]).then_inc(s_ffw, 16)
            for h in range(2):
                sp.dma_start(b2[h * E1:(h + 1) * E1, :], A["L1_ffn_b2"]).then_inc(s_ffw, 16)
            sp.wait_ge(layers[1]["x_done"], FGROUPS)
            sp.dma_start(out_dram, x[:].rearrange("p (t d) -> p t d", d=P)).then_inc(s_out, 16)
            sp.wait_ge(s_out, 16)

        N_SMALL = [9 * 16, 11 * 16]

        @block.tensor
        def _(pe):
            ident = cst[:, C_ID:C_ID + P]

            def attention(L):
                S = layers[L]
                pe.wait_ge(s_setup, 3)
                pe.wait_ge(S["weights"], N_SMALL[L])
                if L:
                    pe.wait_ge(layers[0]["x_done"], FGROUPS)

                def step(j, par, n, f, m, v, b, c, r, k):
                    F, M, V, B, C, K = j - 1, j - 2, j - 3, j - 4, j - 5, j - 7
                    odd = 1 - par

                    def peeled(*js):
                        return isinstance(j, int) and j in js

                    def scores(u):
                        if u == 0:
                            pe.wait_ge(S["k_done"], M + 1)
                            pe.wait_ge(S["q_masked"], M + 1)
                        if not first(M, 0):
                            pe.wait_ge(S["probs"], M * 4 + (u - 3))
                        rows = slice(32 * u, 32 * u + 32)
                        for bb in range(GB):
                            for p in range(2):
                                c = (bb * 2 + p) * SEQ
                                mm = pe.matmul(score[u][:, c:c + SEQ], qm[rows, par, bb, 2 * p:2 * p + 2, :],
                                               kr[rows, par, bb * SEQ:(bb + 1) * SEQ],
                                               start=(bb == 0 and p == 0), stop=False, skip_group_check=True)
                        if L == 0:
                            mm = pe.matmul(score[u][:, :], idb[:], band[:].unsqueeze(1).to_broadcast([P, 8, 64]),
                                           start=False, stop=False, skip_group_check=True)
                        mm.then_inc(S["scores"], 1)

                    def shift(u):
                        pe.wait_ge(S["max_done"], M * 4 + (u + 1))
                        pe.matmul(score[u][:, :], idr[:], nmax[:, u, :].unsqueeze(2).to_broadcast([P, 8, 64]),
                                  start=False, stop=True, skip_group_check=True).then_inc(S["shifted"], 1)

                    def turn(u):
                        pe.wait_ge(S["probs"], V * 4 + (u + 1))
                        w = (w0, w3, w3, w3)[u]
                        if u == 0 and not (isinstance(j, int) and j < 8):
                            pe.wait_ge(S["rt_copied"], K)
                        elif u == 0:
                            pe.wait_ge(S["k_read"], j - 1)
                        for bb in range(GB):
                            mm = pe.transpose(w[:, bb * P:(bb + 1) * P], work[:, u, bb * P:(bb + 1) * P], ident)
                        mm.then_inc(S["pt"], 1)

                    def values(u):
                        pe.wait_ge(S["pt_copied"], V * 4 + (u + 1))
                        w = w2
                        if u == 0:
                            pe.wait_ge(S["v_done" if L else "v_masked"], V + 1)
                        if not (u == 0 and first(V, 0)):
                            pe.wait_ge(S["o_done"], V * 4 + u)
                        for bb in range(GB):
                            mm = pe.matmul(w[:, bb * VW:(bb + 1) * VW], work2[:, u % 2, bb * P:(bb + 1) * P],
                                           vm[:, odd, bb, u, :], start=True, stop=True)
                        mm.then_inc(S["op"], 1)

                    def turn_x():
                        pe.wait_ge(S["xn"], F + 1)
                        if not v and not first(F, 0):
                            pe.wait_ge(S["k_read"], F)
                        for t in range(2):
                            mm = pe.transpose(w0[:, t * P:(t + 1) * P], xn[:, odd, t, :], ident)
                        mm.then_inc(S["xt"], 1)

                    def project(n, w, rhs, done):
                        for h in range(2 - L):
                            mm = pe.matmul(w[:, h * GTOK:(h + 1) * GTOK], wq[:, n, h * P:(h + 1) * P], rhs,
                                           start=True, stop=True)
                        mm.then_inc(done, 1)

                    def project_q():
                        pe.wait_ge(S["xt_copied"], F + 1)
                        project(0, w0, xnT[:, odd, :], S["qp"])

                    def project_k():
                        pe.wait_ge(S["ctx"][odd], (F - odd) * 16 + 32)
                        pe.wait_ge(S["q_read"], F + 1)
                        project(1, w0, ctxT[:, odd, :, 0, :], S["kp"])

                    def project_v():
                        if c:
                            pe.wait_ge(S["lg_read"], C + 1)
                        elif b:
                            pe.wait_ge(S["resid"], B + 1)
                        elif not first(F, 0):
                            pe.wait_ge(S["v_masked"], F)
                        for bb in range(GB):
                            mm = pe.matmul(w1[:, bb * P:(bb + 1) * P], ctxT[:, odd, bb, :, :], wv[:], start=True, stop=True)
                        mm.then_inc(S["vp"], 1)

                    def back_attn():
                        pe.wait_ge(S["o_done"], B * 4 + 4)
                        if peeled(GROUPS + 2, GROUPS + 3):
                            pe.wait_ge(S["lg_read"], C)
                        else:
                            pe.wait_ge(S["v_masked"], j - 1)
                        for bb in range(GB):
                            mm = pe.matmul(w1[:, bb * SEQ:(bb + 1) * SEQ], on[:, par, bb, :], cst[:, C_ID2:C_ID2 + 64],
                                           start=True, stop=True)
                        mm.then_inc(S["at"], 1)

                    def back_out():
                        pe.wait_ge(S["at_copied"], B + 1)
                        for t in range(2):
                            mm = pe.matmul(w1[:, t * P:(t + 1) * P], aT[:, t * P:(t + 1) * P], wo[:], start=True, stop=True)
                        mm.then_inc(S["y"], 1)

                    def back_turn():
                        pe.wait_ge(S["xn2"], C + 1)
                        if b:
                            pe.wait_ge(S["resid"], B + 1)
                        else:
                            pe.wait_ge(S["lg_read"], C)
                        for t in range(2):
                            mm = pe.transpose(w1[:, t * P:(t + 1) * P], xn2[:, t, :], ident)
                        mm.then_inc(S["x2t"], 1)

                    def back_logits():
                        pe.wait_ge(S["x2t_copied"], C + 1)
                        E = (E0, E1)[L]
                        for t in range(2):
                            mm = pe.matmul(w1[:, t * E:(t + 1) * E], ysb[:, t * P:(t + 1) * P], wr[:, 0:E], start=True, stop=True)
                        mm.then_inc(S["lg"], 1)

                    def back_weights():
                        E = (E0, E1)[L]
                        pe.wait_ge(S["route_v"], K + 1)
                        if f:
                            pe.wait_ge(S["k_read"], F + 1)
                        elif not v:
                            pe.wait_ge(S["rt_copied"], K)
                        for t in range(2):
                            mm = pe.transpose(w0[0:2 * E, t * P:(t + 1) * P], rw[:, t * 2 * E:(t + 1) * 2 * E], ident)
                        mm.then_inc(S["rt"], 1)

                    if m: scores(0)
                    if v: turn(0)
                    if b: back_attn()
                    if m: scores(1)
                    if v: values(0); turn(1)
                    if m: shift(0)
                    if b: back_out()
                    if f: turn_x()
                    if m: scores(2)
                    if v: values(1); turn(2)
                    if m: shift(1)
                    if f: project_q()
                    if c: back_turn()
                    if m: scores(3)
                    if v: values(2); turn(3)
                    if m: shift(2)
                    if f: project_k()
                    if c: back_logits()
                    if v: values(3)
                    if m: shift(3)
                    if f: project_v()
                    if k: back_weights()

                slots(pe, step)

            def mixture(L):
                S = layers[L]
                chunks, routed, lag = CHUNKS[L], ROUTED[L], DLAG[L]
                pe.wait_ge(s_ffw, (2 * 16, 6 * 16)[L])
                pe.wait_ge(s_sel, 16 * (L + 1))
                pe.wait_ge(S["x2_kept"], GROUPS)
                pe.wait_ge(S["rt_copied"], GROUPS)
                pe.wait_ge(S["x2t_copied"], GROUPS)
                pe.wait_ge(S["o_done"], GROUPS * 4)

                def split_product(out, w, x, start, stop):
                    (wh, wl), (xh, xl) = w, x
                    pe.matmul(out, wh, xh, start=start, stop=False, skip_group_check=True)
                    pe.matmul(out, wh, xl, start=False, stop=False, skip_group_check=True)
                    return pe.matmul(out, wl, xh, start=False, stop=stop, skip_group_check=True)

                def parts(c, column):
                    return [wsplits[L][:, c % RING[L], a, column * P:(column + 1) * P] for a in range(2)]

                def down(g, c, ring):
                    pe.wait_ge(S["h_lo"], g * chunks + (c + 1))
                    if c == 0:
                        if not first(g, 0):
                            pe.wait_ge(S["y_copied"], g)
                        if L:
                            pe.matmul(bank[6][:, :], b2[:], xin[0:2 * E1, ring, 2, :].bitcast(F32), start=True, stop=False,
                                      skip_group_check=True)
                    slot = ring * chunks + c
                    split_product(bank[6][:, :], parts(slot, 2 - L), [hsplit[:, c % 2, a, :] for a in range(2)],
                                  c == 0 and L == 0, c == chunks - 1).then_inc(S["down"], 1)

                def turn_back(g):
                    pe.wait_ge(S["y_copied"], g + 1)
                    if not first(g, 0):
                        pe.wait_ge(S["x_done"], g)
                    for t in range(4):
                        mm = pe.transpose(bank[7][:, t * P:(t + 1) * P], ysb[:, t * P:(t + 1) * P], cst[:, C_ID:C_ID + P])
                    mm.then_inc(S["yt"], 1)

                def group(g, u):
                    k0 = g * chunks
                    x_parts = [xin[:, u, a, :] for a in range(2)]
                    for c in range(chunks):
                        used = not first(g, 0) or c >= 2
                        slot = u * chunks + c
                        if c == 0:
                            pe.wait_ge(S["x_lo"], g + 1)
                        pe.wait_ge(S["w_lo"], k0 + (c + 1))
                        if used:
                            pe.wait_ge(S["act"], k0 + (c - 1))
                        split_product(bank[c % 2][:, :], parts(slot, 0), x_parts, True, True).then_inc(S["gate"], 1)
                        if L == 0:
                            if used:
                                pe.wait_ge(S["prod"], k0 + (c - 1))
                            split_product(bank[2 + c % 2][:, :], parts(slot, 1), x_parts, True, True).then_inc(S["up"], 1)
                        if c < routed:
                            if used:
                                pe.wait_ge(S["hid"], k0 + (c - 1))
                            if L == 0:
                                strip = slice(c // (routed // 4) * 32, c // (routed // 4) * 32 + 32)
                                cols = c % (routed // 4) * P
                            else:
                                strip, cols = slice(0, 2 * E1), c // (F1 // P) * P
                            pe.matmul(bank[4 + c % 2][:, :], sel[strip, cols:cols + P], xin[strip, u, 2, :],
                                      start=True, stop=True).then_inc(S["spread"], 1)
                        if c >= lag:
                            down(g, c - lag, u)
                        elif not first(g, 0):
                            down(g - 1, chunks - lag + c, 1 - u)
                        if c == lag + 1 and not first(g, 0):
                            turn_back(g - 1)

                pairs(pe, group)
                for c in range(chunks - lag, chunks):
                    down(FGROUPS - 1, c, 1)
                turn_back(FGROUPS - 1)

            for L in range(2):
                attention(L)
                mixture(L)

        @block.scalar
        def _(act):
            for L in range(2):
                S = layers[L]
                E = (E0, E1)[L]
                act.wait_ge(S["weights"], N_SMALL[L])
                act.activation(gates[:], gates[:], ACT.Tanh).then_inc(S["tanh"], 1)

                scale = (HD ** 0.5, HD ** -0.5)[L]

                def step(j, par, n, f, m, v, b, c, r, k):
                    F, M, V, B, C, K = j - 1, j - 2, j - 3, j - 4, j - 5, j - 7
                    odd = 1 - par

                    def load_context():
                        if not (first(j, 0) or first(j, 1)):
                            act.wait_ge(S["vp"], j - 1)
                        src = A["ctxT"][:, bass.ds(j * GTOK, GTOK)].rearrange("d (b s) -> d b s", s=SEQ)
                        for u in range(2):
                            act.dma_start(ctxT[:, par, :, u, :], src).then_inc(S["ctx"][par], 16)

                    def copy_turned(u):
                        act.wait_ge(S["pt"], V * 4 + (u + 1))
                        act.activation(work2[:, u % 2, :], (w0, w3, w3, w3)[u][:, :], ACT.Copy).then_inc(S["pt_copied"], 1)

                    def exps(u):
                        act.wait_ge(S["shifted"], M * 4 + (u + 1))
                        act.activation(work[:, u, :], score[u][:, :], ACT.Exp, scale=scale).then_inc(S["probs"], 1)

                    def keep_weights():
                        act.wait_ge(S["rt"], K + 1)
                        act.activation(rwT[0:2 * E, bass.ds(K * GTOK, GTOK)], w0[0:2 * E, 0:GTOK], ACT.Copy).then_inc(S["rt_copied"], 1)

                    def copy_attn():
                        act.wait_ge(S["at"], B + 1)
                        act.activation(aT[:], w1[:, 0:GTOK], ACT.Copy).then_inc(S["at_copied"], 1)

                    def copy_xn():
                        act.wait_ge(S["xt"], F + 1)
                        act.activation(xnT[:, odd, :], w0[:, 0:GTOK], ACT.Copy).then_inc(S["xt_copied"], 1)

                    def copy_xn2():
                        if isinstance(C, int) and C > 0:
                            act.wait_ge(S["x2_kept"], C)
                        act.wait_ge(S["x2t"], C + 1)
                        act.activation(ysb[:, 0:GTOK], w1[:, 0:GTOK], ACT.Copy).then_inc(S["x2t_copied"], 1)

                    def mask_queries():
                        if L == 0:
                            act.wait_ge(S["q_roped"], F + 1)
                        else:
                            act.wait_ge(S["qp"], F + 1)
                            if first(F, 0):
                                act.wait_ge(S["prep"], 1)
                        for h in range(4):
                            if L == 0:
                                a = act.activation(qm[:, odd, :, h, :], qr[:].rearrange("p (b s) -> p b s", s=SEQ), ACT.Copy,
                                                   scale=cst[:, C_HM + h:C_HM + h + 1])
                            else:
                                a = act.activation(qm[:, odd, :, h, :], w0[:, 0:GTOK].rearrange("p (b s) -> p b s", s=SEQ), ACT.Identity,
                                                   bias=bq4[:, h:h + 1], scale=cst[:, C_HM + h:C_HM + h + 1])
                        a.then_inc(S["q_masked"], 1)

                    def read_logits():
                        if L == 1 and not first(C, 0):
                            act.wait_ge(S["p2v"], C)
                        act.wait_ge(S["lg"], C + 1)
                        if L == 0:
                            act.activation(sg[:], w1[:, 0:2 * E0], ACT.Exp, scale=-1.0).then_inc(S["lg_read"], 1)
                        else:
                            act.activation(sg[:, 0:2 * E1], w1[:, 0:2 * E1], ACT.Copy).then_inc(S["lg_read"], 1)

                    def keep_xn2():
                        act.wait_ge(S["x2t_copied"], C + 1)
                        act.activation(xn2T[:, bass.ds(C * GTOK, GTOK)], ysb[:, 0:GTOK], ACT.Copy).then_inc(S["x2_kept"], 1)

                    if n: load_context()
                    if v: copy_turned(0)
                    if b: copy_attn()
                    if v: copy_turned(1)
                    if m: exps(0)
                    if f: copy_xn()
                    if v: copy_turned(2)
                    if m: exps(1)
                    if f and L == 1: mask_queries()
                    if c: copy_xn2()
                    if v: copy_turned(3)
                    if m: exps(2)
                    if c: read_logits(); keep_xn2()
                    if f and L == 0: mask_queries()
                    if m: exps(3)
                    if k: keep_weights()
                    if c and L == 1:
                        act.wait_ge(S["v2a"], C + 1)
                        act.activation(sc[:, 0:2 * E1], choice[:, 0:2 * E1], ACT.Exp).then_inc(S["a2v"], 1)

                slots(act, step)

                chunks = CHUNKS[L]
                last = FGROUPS * chunks

                act.wait_ge(s_ffw, (2 * 16, 6 * 16)[L])
                act.wait_ge(S["x2_kept"], GROUPS)
                act.wait_ge(S["rt_copied"], GROUPS)
                act.wait_ge(S["at"], GROUPS)
                act.wait_ge(S["lg"], GROUPS)

                def split_input(g, u):
                    if not (first(g, 0) or first(g, 1)):
                        act.wait_ge(S["down"], (g - 1) * chunks)
                    act.activation(xin[:, u, 0, :], xn2T[:, bass.ds(g * FTOK, FTOK)], ACT.Copy).then_inc(S["x_hi"], 1)
                    act.activation(xin[0:2 * E, u, 2, :], rwT[0:2 * E, bass.ds(g * FTOK, FTOK)].bitcast(F32), ACT.Copy).then_inc(S["x_hi"], 1)

                def split_weights(n, c, slot):
                    if not (isinstance(n, int) and n < RING[L]):
                        act.wait_ge(S["down"], n - (RING[L] - 1))
                    act.activation(wsplits[L][:, slot % RING[L], 0, 0:CW[L]], weights[:, c * CW[L]:(c + 1) * CW[L]],
                                   ACT.Copy).then_inc(S["w_hi"], 1)

                def split_hidden(n, c):
                    act.wait_ge(S["hid"], n + 1)
                    if not (isinstance(n, int) and n < 2):
                        act.wait_ge(S["down"], n - 1)
                    act.activation(hsplit[:, c % 2, 0, :], work2[:, c % 2, :], ACT.Copy).then_inc(S["h_hi"], 1)

                def copy_sum(g):
                    act.wait_ge(S["down"], (g + 1) * chunks)
                    if not first(g, 0):
                        act.wait_ge(S["yt"], g)
                    act.activation(ysb[:], bank[6][:, :], ACT.Copy).then_inc(S["y_copied"], 1)

                def group(g, u):
                    k0 = g * chunks
                    if first(g, 0):
                        split_input(g, u)
                        for c in range(AHEAD[L]):
                            split_weights(c, c, c)
                    for c in range(chunks):
                        if c + AHEAD[L] < chunks or not first(g, FGROUPS - 1):
                            split_weights(k0 + (c + AHEAD[L]), (c + AHEAD[L]) % chunks, u * chunks + c + AHEAD[L])
                        if c == DLAG[L] and not first(g, 0):
                            copy_sum(g - 1)
                        act.wait_ge(S["gate"], k0 + (c + 1))
                        if not first(g, 0) or c >= 2:
                            act.wait_ge(S["hid" if L else "prod"], k0 + (c - 1))
                        if L == 0:
                            act.activation(work[:, c % 2, :], bank[c % 2][:, :], ACT.Silu).then_inc(S["act"], 1)
                        else:
                            act.activation(work[:, c % 2, :], bank[c % 2][:, :], ACT.Gelu_apprx_tanh,
                                           bias=b1[:, c:c + 1]).then_inc(S["act"], 1)
                        if not first(g, 0) or c >= 1:
                            split_hidden(k0 + (c - 1), c - 1)
                        if c == chunks // 2 and not first(g, FGROUPS - 1):
                            split_input(g + 1, 1 - u)

                pairs(act, group)
                split_hidden(last - 1, chunks - 1)
                copy_sum(FGROUPS - 1)

        @block.vector
        def _(dve):
            dve.wait_ge(s_const, 16)
            dve.tensor_copy(idr[:], cst[:, C_ID:C_ID + P]).then_inc(s_setup, 1)
            dve.tensor_copy(idb[:], cst[:, C_ID:C_ID + P]).then_inc(s_setup, 1)
            dve.tensor_copy(band[:], cst[:, C_BAND:C_BAND + 64]).then_inc(s_setup, 1)
            dve.wait_ge(s_x, 64)
            dve.tensor_copy(vm[:, :, :, :, 32:34].rearrange("p a b s c -> p (a b s) c"),
                            cst[:, C_JM:C_JM + 2].unsqueeze(1).to_broadcast([P, 2 * GB * STRIPS, 2])).then_inc(s_ones, 1)

            for L in range(2):
                S = layers[L]
                E = (E0, E1)[L]
                dve.wait_ge(S["tanh"], 1)
                dve.tensor_scalar(gbo[:], brow[:, 0, :], gates[:, L:L + 1], None, ALU.mult)
                if L:
                    dve.tensor_tensor(bvm[:].rearrange("p (s c) -> p s c", c=32), brow[:, 1, :].rearrange("p (s c) -> p s c", c=32),
                                      cst[:, C_VM:C_VM + 32].unsqueeze(1).to_broadcast([P, 4, 32]), ALU.mult)
                dve.tensor_scalar(bq4[:], cst[:, C_HM:C_HM + 4], bcol[:, 0:1] if L else 0.0, None, ALU.mult).then_inc(S["prep"], 1)

                def step(j, par, n, f, m, v, b, c, r, k):
                    F, M, V, B, C, R = j - 1, j - 2, j - 3, j - 4, j - 5, j - 6
                    odd = 1 - par

                    def norm_stats():
                        for t in range(2):
                            a = dve.bn_stats(st[:, par, t, :], x[:, bass.ds(j * GTOK + t * P, P)])
                        a.then_inc(S["stats"], 1)
                        hold(dve, S["stats"], j + 1)
                        for t in range(2):
                            a = dve.bn_aggr(mv[:, par, t, :], st[:, par, t, :])
                        a.then_inc(S["varp"], 1)

                    def norm_apply():
                        dve.wait_ge(S["rstd"], j * 2 + 2)
                        for t in range(2):
                            a = dve.tensor_scalar(xn[:, par, t, :], x[:, bass.ds(j * GTOK + t * P, P)],
                                                  mv[:, par, t, 0:1], rs[:, par, t:t + 1], ALU.subtract, ALU.mult)
                        a.then_inc(S["xn"], 1)

                    def max_rows(u):
                        dve.wait_ge(S["scores"], M * 4 + (u + 1))
                        dve.tensor_reduce(nmax[:, u, :], score[u][:].rearrange("p (a k) -> p a k", k=SEQ), AX.X, ALU.max,
                                          negate=True).then_inc(S["max_done"], 1)

                    def outs(u):
                        w = w2
                        dve.wait_ge(S["op"], V * 4 + (u + 1))
                        o = w[:, 0:GB * VW].rearrange("p (b c) -> p b c", c=VW)
                        dve.reciprocal(rden[:, odd, :, :], o[:, :, 32:34]).then_inc(S["rden"], 1)
                        dve.wait_ge(S["rden"], V * 4 + (u + 1))
                        dve.tensor_tensor(rdm[:, odd, :, :, :], rden[:, odd, :, :].unsqueeze(3).to_broadcast([P, GB, 2, 2]),
                                          cst[:, C_JM:C_JM + 2].unsqueeze(1).unsqueeze(1).to_broadcast([P, GB, 2, 2]),
                                          ALU.mult).then_inc(S["rdm"], 1)
                        dve.wait_ge(S["rdm"], V * 4 + (u + 1))
                        dve.tensor_tensor(on[:, odd, :, 32 * u:32 * u + 32].rearrange("p b (h d) -> p b h d", d=HD),
                                          o[:, :, 0:32].rearrange("p b (h d) -> p b h d", d=HD),
                                          rdm[:, odd, :, :, :].rearrange("p b q r -> p b (q r)").unsqueeze(3).to_broadcast([P, GB, 4, HD]),
                                          ALU.mult).then_inc(S["o_done"], 1)

                    def rotate(n, w, ready, read):
                        dve.wait_ge(ready, F + 1)
                        if n == 0:
                            if not first(F, 0):
                                dve.wait_ge(S["q_roped"], F)
                        else:
                            if not first(F, 0):
                                dve.wait_ge(S["k_done"], F)
                        for h in range(2):
                            a = dve.tensor_tensor(rope[:, 2 * n + h, :].rearrange("p (b s) -> p b s", s=SEQ),
                                                  w[:, h * GTOK:(h + 1) * GTOK].rearrange("p (b s) -> p b s", s=SEQ),
                                                  cst[:, C_COS + 64 * h:C_COS + 64 * h + 64].unsqueeze(1).to_broadcast([P, GB, 64]),
                                                  ALU.mult)
                        a.then_inc(read, 1)

                    def mask_values():
                        dve.wait_ge(S["vp"], F + 1)
                        dve.tensor_tensor(vm[:, odd, :, :, 0:32],
                                          w1[:].rearrange("p (b s c) -> p b s c", b=GB, c=32),
                                          cst[:, C_VM:C_VM + 32].unsqueeze(1).unsqueeze(1).to_broadcast([P, GB, 4, 32]),
                                          ALU.mult).then_inc(S["v_masked"], 1)

                    def residual():
                        dve.wait_ge(S["y"], B + 1)
                        dve.wait_ge(S["xb"], B + 1)
                        xs = x[:, bass.ds(B * GTOK, GTOK)]
                        dve.scalar_tensor_tensor(xs, w1[:, 0:GTOK], gates[:, L:L + 1], xb[:, par, :], ALU.mult, ALU.add).then_inc(S["resid"], 1)
                        hold(dve, S["resid"], B + 1)
                        for t in range(2):
                            a = dve.bn_stats(st2[:, t, :], x[:, bass.ds(B * GTOK + t * P, P)])
                        a.then_inc(S["stats2"], 1)
                        hold(dve, S["stats2"], B + 1)
                        for t in range(2):
                            a = dve.bn_aggr(mv2[:, par, t, :], st2[:, t, :])
                        a.then_inc(S["varp2"], 1)

                    def norm2_apply():
                        dve.wait_ge(S["rstd2"], C * 2 + 2)
                        for t in range(2):
                            a = dve.tensor_scalar(xn2[:, t, :], x[:, bass.ds(C * GTOK + t * P, P)],
                                                  mv2[:, odd, t, 0:1], rs2[:, odd, t:t + 1], ALU.subtract, ALU.mult)
                        a.then_inc(S["xn2"], 1)

                    def score_one():
                        dve.wait_ge(S["lg_read"], C + 1)
                        dve.tensor_scalar(sc[:], sg[:], 1.0, None, ALU.add).then_inc(S["v2a"], 1)

                    def score_two():
                        dve.wait_ge(S["v2a"], C * 3 + 1)
                        dve.reciprocal(sc[:], sc[:]).then_inc(S["v2a"], 1)

                    def score_three():
                        dve.wait_ge(S["v2a"], C * 3 + 2)
                        dve.tensor_tensor(choice[:].rearrange("p (t e) -> p t e", e=E0), sc[:].rearrange("p (t e) -> p t e", e=E0),
                                          brow[:, 1, 0:E0].unsqueeze(1).to_broadcast([P, 2, E0]), ALU.add).then_inc(S["v2a"], 1)

                    def score_four():
                        hold(dve, S["v2a"], C * 3 + 3)
                        for g in range(16):
                            a = dve.max(gtop[:, g, :], choice[:, g * 8:(g + 1) * 8])
                        a.then_inc(S["v2p"], 1)

                    def score_logits():
                        lg = sg[:, 0:2 * E1].rearrange("p (t e) -> p t e", e=E1)
                        dve.wait_ge(S["lg_read"], C + 1)
                        dve.tensor_reduce(top8[:, 0, 0:2], lg, AX.X, ALU.max).then_inc(S["v2p"], 1)
                        dve.wait_ge(S["v2p"], C + 1)
                        dve.tensor_tensor(choice[:, 0:2 * E1].rearrange("p (t e) -> p t e", e=E1), lg,
                                          top8[:, 0, 0:2].unsqueeze(2).to_broadcast([P, 2, E1]), ALU.subtract).then_inc(S["v2a"], 1)

                    ws = wsel[:, 0:2 * E]
                    wt = ws.rearrange("p (t e) -> p t e", e=E)
                    kept = rwr[:, 0:2 * E]
                    links = (8, 5)[L]

                    def pick_one():
                        hold(dve, S["p2v"], R + 1)
                        for t in range(2):
                            a = dve.max(top8[:, t, :], masked[:, t * E:(t + 1) * E])
                        a.then_inc(S["chain"], 1)

                    def pick_two():
                        hold(dve, S["chain"], R * links + 1)
                        for t in range(2):
                            a = dve.match_replace(rest[:, t * E:(t + 1) * E], top8[:, t, :], masked[:, t * E:(t + 1) * E], MASKED)
                        a.then_inc(S["chain"], 1)

                    def pick_three():
                        dve.wait_ge(S["chain"], R * links + 2)
                        dve.scalar_tensor_tensor(ws, rest[:], MASKED * 0.5, sc[:], ALU.is_lt, ALU.mult).then_inc(S["chain"], 1)

                    def pick_best_two():
                        dve.wait_ge(S["a2v"], R + 1)
                        dve.wait_ge(S["p2v"], R + 1)
                        dve.tensor_tensor(ws, sc[:, 0:2 * E], masked[:, 0:2 * E], ALU.mult).then_inc(S["chain"], 1)

                    def weigh_one():
                        dve.wait_ge(S["chain"], R * links + links - 4 - (L == 0))
                        dve.tensor_reduce(wsum[:], wt, AX.X, ALU.add).then_inc(S["chain"], 1)

                    def weigh_two():
                        if L == 0:
                            dve.wait_ge(S["chain"], R * links + links - 4)
                            dve.tensor_scalar(wsum[:], wsum[:], 1e-20, None, ALU.add).then_inc(S["chain"], 1)

                    def weigh_three():
                        dve.wait_ge(S["chain"], R * links + links - 3)
                        dve.reciprocal(wsum[:], wsum[:]).then_inc(S["chain"], 1)

                    def weigh_four():
                        hold(dve, S["chain"], R * links + links - 2)
                        dve.scalar_tensor_tensor(wt, wt, (RSCALE, 1.0)[L], wsum[:].unsqueeze(2).to_broadcast([P, 2, E]),
                                                 ALU.mult, ALU.mult).then_inc(S["chain"], 1)

                    def weigh_five():
                        dve.wait_ge(S["chain"], R * links + links - 1)
                        dve.tensor_copy(kept, ws).then_inc(S["chain"], 1)

                    def weigh_six():
                        strip = (STRIP_E, E1)[L]
                        parts = rw[:, 0:4 * E].rearrange("p (t a e) -> p t a e", a=2, e=strip)
                        dve.wait_ge(S["chain"], R * links + links)
                        if not first(R, 0):
                            dve.wait_ge(S["rt"], R)
                        dve.tensor_copy(parts[:, :, 0, :], kept.bitcast(F32).rearrange("p (t e) -> p t e", e=strip))
                        dve.tensor_tensor(parts[:, :, 1, :], ws.rearrange("p (t e) -> p t e", e=strip),
                                          kept.bitcast(F32).rearrange("p (t e) -> p t e", e=strip),
                                          ALU.subtract).then_inc(S["route_v"], 1)

                    def bias_keys():
                        dve.wait_ge(S["kp"], F + 1)
                        dve.tensor_scalar(kr[:, odd, :], w0[:, 0:GTOK], bcol[:, 1:2], None, ALU.add).then_inc(S["k_done"], 1)

                    if c: norm2_apply()
                    if m: max_rows(0)
                    if n: norm_stats()
                    if m: max_rows(1)
                    if v: outs(0)
                    if b: residual()
                    if m: max_rows(2)
                    if v: outs(1)
                    if r and L == 0: pick_one()
                    if f and L == 0: rotate(0, w0, S["qp"], S["q_read"])
                    if r and L == 0: pick_two()
                    if m: max_rows(3)
                    if r and L == 0: pick_three()
                    if r and L == 1: pick_best_two()
                    if v: outs(2)
                    if r: weigh_one()
                    if f and L == 0: rotate(1, w0, S["kp"], S["k_read"])
                    if f and L == 1: bias_keys()
                    if r: weigh_two()
                    if c and L == 0: score_one()
                    if c and L == 1: score_logits()
                    if r: weigh_three()
                    if v: outs(3)
                    if r: weigh_four()
                    if c and L == 0: score_two()
                    if r: weigh_five()
                    if f: mask_values()
                    if r: weigh_six()
                    if c and L == 0: score_three()
                    if n: norm_apply()
                    if c and L == 0: score_four()

                slots(dve, step)

                chunks, routed = CHUNKS[L], ROUTED[L]
                dve.wait_ge(S["pt_copied"], GROUPS * 4)

                def split_input(g, u):
                    dve.wait_ge(S["x_hi"], g * 2 + 2)
                    dve.tensor_tensor(xin[:, u, 1, :], xn2T[:, bass.ds(g * FTOK, FTOK)], xin[:, u, 0, :].bitcast(F32),
                                      ALU.subtract).then_inc(S["x_lo"], 1)

                def split_hidden(n, c):
                    dve.wait_ge(S["h_hi"], n + 1)
                    dve.tensor_tensor(hsplit[:, c % 2, 1, :], work2[:, c % 2, :], hsplit[:, c % 2, 0, :].bitcast(F32),
                                      ALU.subtract).then_inc(S["h_lo"], 1)

                def add_sum(g):
                    dve.wait_ge(S["yt"], g + 1)
                    xs = x[:, bass.ds(g * FTOK, FTOK)]
                    dve.scalar_tensor_tensor(xs, bank[7][:, :], gates[:, 2 + L:3 + L], xs, ALU.mult, ALU.add).then_inc(S["x_done"], 1)

                def group(g, u):
                    k0 = g * chunks
                    if first(g, 0):
                        split_input(g, u)
                    for c in range(chunks):
                        held = work2[:, c % 2, :]
                        if L == 0:
                            dve.wait_ge(S["act"], k0 + (c + 1))
                            dve.wait_ge(S["up"], k0 + (c + 1))
                            dve.tensor_tensor(work[:, 2 + c % 2, :], work[:, c % 2, :], bank[2 + c % 2][:, :],
                                              ALU.mult).then_inc(S["prod"], 1)
                            dve.wait_ge(S["prod"], k0 + (c + 1))
                        else:
                            dve.wait_ge(S["act"], k0 + (c + 1))
                        if not first(g, 0) or c >= 2:
                            dve.wait_ge(S["h_lo"], k0 + (c - 1))
                        if c < routed:
                            dve.wait_ge(S["spread"], g * routed + (c + 1))
                            dve.tensor_tensor(held, work[:, (2 + c % 2, c % 2)[L], :], bank[4 + c % 2][:, :],
                                              ALU.mult).then_inc(S["hid"], 1)
                        else:
                            dve.tensor_copy(held, work[:, 2 + c % 2, :]).then_inc(S["hid"], 1)
                        if not first(g, 0) or c >= 1:
                            split_hidden(k0 + (c - 1), c - 1)
                        if c == 5 and not first(g, 0):
                            add_sum(g - 1)
                        if c == chunks // 2 and not first(g, FGROUPS - 1):
                            split_input(g + 1, 1 - u)

                pairs(dve, group)
                split_hidden(FGROUPS * chunks - 1, chunks - 1)
                add_sum(FGROUPS - 1)
                dve.wait_ge(S["x_done"], FGROUPS)

        @block.gpsimd
        def _(pool):
            pool.memset(mhalf[:], -0.5).then_inc(s_half, 1)
            pool.dma_start(sel[:], A["sel0"]).then_inc(s_sel, 16)
            pool.wait_ge(s_half, 1)
            for L in range(2):
                S = layers[L]
                pool.wait_ge(S["prep"], 1)
                if L:
                    pool.dma_start(sel1, A["sel1"]).then_inc(s_sel, 16)

                def step(j, par, n, f, m, v, b, c, r, k):
                    F, V, B, R = j - 1, j - 3, j - 4, j - 6
                    odd = 1 - par

                    def add_bias():
                        if not (first(V, 0) or first(V, 1)):
                            pool.wait_ge(S["resid"], V - 1)
                        pool.tensor_tensor(xb[:, odd, :].rearrange("p (t d) -> p t d", d=P),
                                           x[:, bass.ds(V * GTOK, GTOK)].rearrange("p (t d) -> p t d", d=P),
                                           gbo[:].unsqueeze(1).to_broadcast([P, 2, P]), ALU.add).then_inc(S["xb"], 1)

                    def deviation(varp, rstd, group, var, plus, inverse):
                        hold(pool, varp, group + 1)
                        pool.tensor_scalar(plus, var, EPS, None, ALU.add).then_inc(rstd, 1)
                        pool.wait_ge(rstd, group * 2 + 1)
                        pool.tensor_tensor(inverse, plus, mhalf[:], ALU.pow).then_inc(rstd, 1)

                    def rope_queries():
                        pool.wait_ge(S["q_read"], F + 1)
                        if not first(F, 0):
                            pool.wait_ge(S["q_masked"], F)
                        pool.tensor_tensor(qr[:], rope[:, 0, :], rope[:, 1, :], ALU.add).then_inc(S["q_roped"], 1)

                    def rope_keys():
                        pool.wait_ge(S["k_read"], F + 1)
                        pool.tensor_tensor(kr[:, odd, :], rope[:, 2, :], rope[:, 3, :], ALU.add).then_inc(S["k_done"], 1)

                    def bias_values():
                        pool.wait_ge(S["v_masked"], F + 1)
                        vals = vm[:, odd, :, :, 0:32]
                        pool.tensor_tensor(vals, vals, bvm[:].rearrange("p (s c) -> p s c", c=32).unsqueeze(1).to_broadcast([P, GB, 4, 32]),
                                           ALU.add).then_inc(S["v_done"], 1)

                    if r and L == 0:
                        pool.wait_ge(S["v2p"], R + 1)
                        route0(R)
                    if r and L == 1:
                        pool.wait_ge(S["lg_read"], R + 1)
                        route1(R)
                    if b: deviation(S["varp2"], S["rstd2"], B, mv2[:, par, :, 1], ve2[:, par, :], rs2[:, par, :])
                    if f and L == 0: rope_queries(); rope_keys()
                    if n: deviation(S["varp"], S["rstd"], j, mv[:, par, :, 1], ve[:, par, :], rs[:, par, :])
                    if v: add_bias()
                    if f and L == 1: bias_values()

                def ranks(link, val):
                    for t in range(2):
                        vj = val[:, t * 8:t * 8 + 8].unsqueeze(1).to_broadcast([P, 8, 8])
                        vi = val[:, t * 8:t * 8 + 8].unsqueeze(2).to_broadcast([P, 8, 8])
                        gt = cmp[:, 0, t * 64:t * 64 + 64].rearrange("p (i j) -> p i j", j=8)
                        eq = cmp[:, 1, t * 64:t * 64 + 64].rearrange("p (i j) -> p i j", j=8)
                        link(pool.tensor_tensor(gt, vj, vi, ALU.subtract))
                        link(pool.tensor_scalar(eq, gt, 0.0, None, ALU.is_equal))
                        link(pool.tensor_scalar(gt, gt, 0.0, None, ALU.is_gt))
                        link(pool.tensor_tensor(eq, eq, cst[:, C_TRI:C_END].rearrange("p (i j) -> p i j", j=8), ALU.mult))
                    link(pool.tensor_tensor(cmp[:, 0, :], cmp[:, 0, :], cmp[:, 1, :], ALU.add))
                    c = cmp[:, 0, :].rearrange("p (i j) -> p i j", j=8)
                    link(pool.tensor_tensor(cmp[:, 1, 0:64].rearrange("p (i j) -> p i j", j=4), c[:, :, 0:4], c[:, :, 4:8], ALU.add))
                    c = cmp[:, 1, 0:64].rearrange("p (i j) -> p i j", j=4)
                    link(pool.tensor_tensor(cmp[:, 0, 0:32].rearrange("p (i j) -> p i j", j=2), c[:, :, 0:2], c[:, :, 2:4], ALU.add))
                    c = cmp[:, 0, 0:32].rearrange("p (i j) -> p i j", j=2)
                    link(pool.tensor_tensor(rank[:], c[:, :, 0], c[:, :, 1], ALU.add))

                def route0(B):
                    n = [0]

                    def link(ins):
                        n[0] += 1
                        ins.then_inc(S["route_p"], 1)
                        hold(pool, S["route_p"], B * 14 + n[0])
                    link(pool.tensor_tensor(gsum[:], gtop[:, :, 0], gtop[:, :, 1], ALU.add))
                    ranks(link, gsum)
                    link(pool.tensor_scalar(rank[:], rank[:], float(TOPG0), None, ALU.is_lt))
                    if not first(B, 0):
                        pool.wait_ge(S["route_v"], B)
                    pool.tensor_tensor(masked[:].rearrange("p (g e) -> p g e", e=8), choice[:].rearrange("p (g e) -> p g e", e=8),
                                       rank[:].unsqueeze(2).to_broadcast([P, 16, 8]), ALU.mult).then_inc(S["p2v"], 1)
                    assert n[0] == 14, n[0]

                def route1(B):
                    n = [0]

                    def link(ins):
                        n[0] += 1
                        ins.then_inc(S["route_p"], 1)
                        hold(pool, S["route_p"], B * 12 + n[0])
                    ranks(link, sg)
                    if not first(B, 0):
                        hold(pool, S["route_v"], B)
                    pool.tensor_scalar(masked[:, 0:16], rank[:], 2.0, None, ALU.is_lt).then_inc(S["p2v"], 1)
                    assert n[0] == 12, n[0]

                slots(pool, step)

                chunks = CHUNKS[L]

                def group(g, u):
                    for c in range(chunks):
                        slot = (u * chunks + c) % RING[L]
                        pool.wait_ge(S["w_hi"], g * chunks + (c + 1))
                        pool.tensor_tensor(wsplits[L][:, slot, 1, 0:CW[L]], weights[:, c * CW[L]:(c + 1) * CW[L]],
                                           wsplits[L][:, slot, 0, 0:CW[L]].bitcast(F32), ALU.subtract).then_inc(S["w_lo"], 1)

                pairs(pool, group)


def kernel(**inputs):
    import concourse.bacc as _bacc
    from concourse.bass_utils import run_bass_kernel_spmd as _run

    I = {k: np.asarray(v) for k, v in inputs.items()}
    swap = np.concatenate([np.arange(64, 128), np.arange(0, 64)])
    a = {"cst": constants(), "x": I["x"]}
    a["sel0"], a["sel1"] = spread_rows()
    a["ctxT"] = I["ctx_1024"].reshape(TOK, D).T
    for n in ("g_xattn", "g_ffn", "L0_ffn_gate_bias", "L1_ffn_b2"):
        a[n] = I[n]
    for s in "qk":
        w = I["L0_xattn_w" + s].T
        a["L0_w" + s] = np.concatenate([w, w[:, swap]], axis=1)
        a["L1_w" + s] = I["L1_xattn_W_" + s]
    a["L0_wv"], a["L1_wv"] = I["L0_xattn_wv"].T, I["L1_xattn_W_v"]
    a["L0_wo"], a["L1_wo"] = I["L0_xattn_wo_w"].T, I["L1_xattn_W_o"]
    a["L0_bo"], a["L1_bo"] = I["L0_xattn_wo_b"], I["L1_xattn_b_o"]
    a["L1_bq"], a["L1_bk"], a["L1_bv"] = I["L1_xattn_b_q"], I["L1_xattn_b_k"], I["L1_xattn_b_v"]
    a["L0_router"], a["L1_router"] = I["L0_ffn_gate_w"].T, I["L1_ffn_Wg"]
    rows = CHUNKS[0] * P
    gate, up, down = np.zeros((3, rows, D), np.float32)
    gate[:ROUTED0], up[:ROUTED0] = I["L0_ffn_Wg"].reshape(ROUTED0, D), I["L0_ffn_Wu"].reshape(ROUTED0, D)
    gate[ROUTED0:ROUTED0 + SHARED], up[ROUTED0:ROUTED0 + SHARED] = I["L0_ffn_Sg"], I["L0_ffn_Su"]
    down[:ROUTED0] = I["L0_ffn_Wd"].transpose(0, 2, 1).reshape(ROUTED0, D)
    down[ROUTED0:ROUTED0 + SHARED] = I["L0_ffn_Sd"].T
    turned = [w.reshape(CHUNKS[0], P, D).transpose(2, 0, 1) for w in (gate, up)]
    a["mix0"] = np.concatenate(turned + [down.reshape(CHUNKS[0], P, D).transpose(1, 0, 2)], axis=2).reshape(P, -1)
    w1 = I["L1_ffn_W1"].transpose(1, 0, 2).reshape(D, CHUNKS[1], P)
    w2 = I["L1_ffn_W2"].reshape(CHUNKS[1], P, D).transpose(1, 0, 2)
    a["mix1"] = np.concatenate([w1, w2], axis=2).reshape(P, -1)
    a["b1"] = I["L1_ffn_b1"].reshape(CHUNKS[1], P).T

    nc = _bacc.Bacc("TRN2", target_bir_lowering=False, num_devices=1)
    arrays, args = {}, {}
    for name, v in a.items():
        v = np.ascontiguousarray(v)
        arrays[f"in_{name}"] = v
        args[name] = nc.dram_tensor(f"in_{name}", v.shape, mybir.dt.from_np(v.dtype), kind="ExternalInput").ap()
    out = nc.dram_tensor("out_0", (BATCH, SEQ, D), F32, kind="ExternalOutput").ap()
    build(nc, args, out)
    r = _run(nc, [arrays], core_ids=[0])
    return r.results[0]["out_0"]
```

```python
import numpy as np
from contextlib import ExitStack

import concourse.bass as bass
from concourse import mybir

ALU = mybir.AluOpType
ACT = mybir.ActivationFunctionType
AX = mybir.AxisListType
F32 = mybir.dt.float32
F32R = mybir.dt.float32r
BF16 = mybir.dt.bfloat16

P = 128
BATCH, SEQ, D = 64, 64, 128
TOK = BATCH * SEQ
HEADS, HD = 16, 8
EPS = 1e-5
MASKED = -1e30

GB = 4
GTOK = GB * SEQ
GROUPS = TOK // GTOK
LAGS = 8
LATE = (GROUPS + LAGS - 3, GROUPS + LAGS - 2)
STRIPS = 4
VW = HD + 1

E0, I0, TOPG0 = 64, 88, 4
SHARED = 176
RSCALE = 2.5
ROUTED0 = E0 * I0
STRIP_E = 16
E1, F1 = 8, 512
ROUTED = (ROUTED0 // P, E1 * F1 // P)
CHUNKS = (ROUTED[0] + -(-SHARED // P), ROUTED[1])
CW = (3 * P, 2 * P)
RING = (4, 8)
AHEAD = (1, 4)
DLAG = (2, 3)
FTOK = 512
FGROUPS = TOK // FTOK

C_ID, C_JM, C_HM, C_COS, C_SIN, C_BAND, C_TRI, C_END = 0, 128, 130, 134, 198, 262, 326, 390


def constants():
    c = np.zeros((P, C_END), np.float32)
    row = np.arange(P)
    c[:, C_ID:C_JM] = np.eye(P)
    c[:, C_JM:C_HM] = (row // 64)[:, None] == np.arange(2)
    c[:, C_HM:C_COS] = ((row % 32) // HD)[:, None] == np.arange(4)
    half = D // 2
    inv = np.float32(1.0) / np.float32(10000.0) ** (np.arange(half, dtype=np.float32) / np.float32(half))
    ang = np.arange(SEQ, dtype=np.float32)[:, None] * inv[None, :]
    cos, sin = np.cos(ang).T, np.sin(ang).T
    c[:, C_COS:C_SIN] = np.concatenate([cos, cos])
    c[:half, C_SIN:C_BAND] -= sin
    c[half:, C_SIN:C_BAND] += sin
    q, k = (row % 64)[:, None], np.arange(64)[None, :]
    c[:, C_BAND:C_TRI] = np.where(abs(q - k) <= 32, 0.0, MASKED)
    i, j = np.arange(8)[:, None], np.arange(8)[None, :]
    c[:, C_TRI:C_END] = (j < i).reshape(1, 64)
    return c


def spread_rows():
    row = np.arange(P)
    sel0 = (row % STRIP_E)[:, None] == (np.arange(STRIP_E * I0) // I0)[None, :]
    sel1 = (np.arange(2 * E1) % E1)[:, None] == (np.arange(E1 * P) // P)[None, :]
    return sel0.astype(np.float32), sel1.astype(np.float32)


def build(nc, A, out):
    x_dram = A["x"].rearrange("b s d -> (b s) d").rearrange("(t p) d -> p t d", p=P)
    out_dram = out.rearrange("b s d -> (b s) d").rearrange("(t p) d -> p t d", p=P)

    with ExitStack() as ctx:
        def sb(name, shape, dt=F32):
            return ctx.enter_context(nc.sbuf_tensor(name, shape, dt))

        def sem(name):
            return ctx.enter_context(nc.semaphore(name))

        bank = [ctx.enter_context(nc.psum_tensor(f"bank{i}", [P, 512], F32)) for i in range(8)]
        score = bank[0:4]
        w0, w1, w2, w3 = bank[4:8]

        x = sb("x", [P, TOK])
        xn2T = sb("xn2T", [P, TOK])
        rwT = sb("rwT", [P, TOK], F32R)
        cst = sb("cst", [P, C_END])
        idr = sb("idr", [P, P], F32R)
        idb = sb("idb", [P, P], BF16)
        band = sb("band", [P, 64], BF16)
        weights = sb("weights", [P, CHUNKS[0] * CW[0]])
        sel = sb("sel", [P, STRIP_E * I0], F32R)
        gates = sb("gates", [P, 4])
        mhalf = sb("mhalf", [P, 2])
        idle = sb("idle", [P, 48])

        wqk = sb("wqk", [P, 2, 2 * P])
        wv = sb("wv", [P, P])
        wo = sb("wo", [P, P])
        wr = sb("wr", [P, E0])
        brow = sb("brow", [P, 2, P])
        bcol = sb("bcol", [P, 2])
        bk4 = sb("bk4", [P, 4])
        b1 = sb("b1", [P, CHUNKS[1]])
        b2 = sb("b2", [2 * E1, P])
        gbo = sb("gbo", [P, P])
        bvm = sb("bvm", [P, P])

        st = sb("st", [P, 2, 2, 6])
        mv = sb("mv", [P, 2, 2, 2])
        ve = sb("ve", [P, 2, 2])
        rs = sb("rs", [P, 2, 2])
        xn = sb("xn", [P, 2, 2, P])
        kr = sb("kr", [P, GTOK])
        vm = sb("vm", [P, 2, GB, HEADS, VW])
        with nc.sbuf_tensor("arena", [P, 6144], F32) as arena:
            ctxT = arena[:, 0:1024].rearrange("p (u b c s) -> p u b c s", u=2, b=GB, c=2)
            xnT = arena[:, 1024:1536].rearrange("p (u n) -> p u n", u=2)
            rope = arena[:, 1536:2560].rearrange("p (u n) -> p u n", u=4)
            km = arena[:, 2560:4608].rearrange("p (u b h s) -> p u b h s", u=2, b=GB, h=4)
            qT = arena[:, 4608:5120].rearrange("p (u n) -> p u n", u=2)
            on = arena[:, 5120:5632].rearrange("p (u t e) -> p u t e", u=2, t=2)
        wring = sb("wring", [P, RING[1] * 2 * CW[1]], F32R)
        wsplits = [wring[:, 0:RING[L] * 2 * CW[L]].rearrange("p (r a n) -> p r a n", r=RING[L], a=2) for L in range(2)]
        hsplit = sb("hsplit", [P, 2, 2, FTOK], F32R)

        nmax = sb("nmax", [P, 4, 8], F32R)
        work = sb("work", [P, 4, 512])
        work2 = sb("work2", [P, 2, 512])
        rden = sb("rden", [P, 2, 2, 4])

        aT = sb("aT", [P, GTOK])
        xb = sb("xb", [P, 2, GTOK])
        st2 = sb("st2", [P, 2, 6])
        mv2 = sb("mv2", [P, 2, 2, 2])
        ve2 = sb("ve2", [P, 2, 2])
        rs2 = sb("rs2", [P, 2, 2])
        xn2 = sb("xn2", [P, 2, P])
        ysb = sb("ysb", [P, FTOK])

        xin = sb("xin", [P, 2, 3, FTOK], F32R)

        sg = sb("sg", [P, 2 * E0])
        sc = sb("sc", [P, 2 * E0])
        choice = sb("choice", [P, 2 * E0])
        gtop = sb("gtop", [P, 16, 8])
        gsum = sb("gsum", [P, 16])
        cmp = sb("cmp", [P, 2, P])
        rank = sb("rank", [P, 16])
        masked = sb("masked", [P, 2 * E0])
        top8 = sb("top8", [P, 2, 8])
        rest = sb("rest", [P, 2 * E0])
        wsel = sb("wsel", [P, 2 * E0])
        wsum = sb("wsum", [P, 2])
        rwr = sb("rwr", [P, 2 * E0], F32R)
        rw = sb("rw", [P, 4 * E0])

        s_const, s_ffw, s_sel, s_out = sem("const_loaded"), sem("mixture_loaded"), sem("spread_loaded"), sem("out_stored")
        s_x = [sem(f"x_loaded{i}") for i in range(4)]
        s_setup, s_half = sem("identities_made"), sem("half_made")

        def layer_semaphores(L):
            names = (
                "weights", "tanh", "prep",
                "stats", "varp", "rstd", "xn", "xt", "xt_copied", "kp", "k_read", "k_roped", "k_masked",
                "qp", "q_read", "q_done", "vp", "v_masked", "v_done",
                "scores", "max_done", "shifted", "probs", "pt", "pt_copied", "op", "rden", "o_done",
                "at", "at_copied", "xb", "y", "resid", "stats2", "varp2", "rstd2", "xn2", "x2t", "x2t_copied",
                "x2_kept", "lg", "lg_read", "route_v", "route_p", "p2v", "v2p", "rt", "rt_copied", "a2v", "v2a", "chain",
                "x_hi", "x_lo", "w_hi", "w_lo", "gate", "up", "spread", "act", "prod", "hid", "h_hi", "h_lo", "down",
                "y_copied", "yt", "x_done")
            S = {name: sem(f"{name}{L}") for name in names}
            S["ctx"] = [sem(f"ctx_loaded{L}_{i}") for i in range(2)]
            if L == 1:
                S["k_read"], S["q_read"] = S["k_masked"], S["q_done"]
            return S

        layers = [layer_semaphores(0), layer_semaphores(1)]

        block = ctx.enter_context(nc.Block())

        def first(value, n):
            return isinstance(value, int) and value == n

        held = {}

        def hold(eng, semaphore, value):
            eng.wait_ge(semaphore, value)
            if not isinstance(value, int):
                n = held.setdefault((eng.engine, semaphore.name), len(held))
                if eng.engine == mybir.EngineType.Pool:
                    eng.tensor_tensor(idle[:, n:n + 1], mhalf[:, 0:1], mhalf[:, 1:2], ALU.add)
                else:
                    eng.tensor_copy(idle[:, n:n + 1], cst[:, 0:1])

        def has_group(j):
            return [0 <= j - lag < GROUPS for lag in range(LAGS)]

        def slots(eng, step):
            for j in range(LAGS):
                step(j, j % 2, *has_group(j))
            with eng.Fori(0, (GROUPS - LAGS) // 2) as i:
                for h in range(2):
                    step(i * 2 + LAGS + h, h, *has_group(LAGS))
            for j in range(GROUPS, LATE[0]):
                step(j, j % 2, *has_group(j))

        def late(step, n):
            j = LATE[n]
            step(j, j % 2, *has_group(j))

        def pairs(eng, group):
            group(0, 0)
            with eng.Fori(0, (FGROUPS - 2) // 2) as i:
                group(i * 2 + 1, 1)
                group(i * 2 + 2, 0)
            group(FGROUPS - 1, 1)

        @block.sync
        def _(sp):
            sp.dma_start(cst[:], A["cst"]).then_inc(s_const, 16)

            def small(L, S):
                pre = f"L{L}_"
                if L == 0:
                    sp.dma_start(gates[:, 0:2], A["g_xattn"].rearrange("(a n) -> a n", a=1).to_broadcast([P, 2])).then_inc(S["weights"], 16)
                    sp.dma_start(gates[:, 2:4], A["g_ffn"].rearrange("(a n) -> a n", a=1).to_broadcast([P, 2])).then_inc(S["weights"], 16)
                for n, s in enumerate(("q", "k")):
                    src = A[pre + "w" + s]
                    sp.dma_start(wqk[:, n, 0:src.shape[1]], src).then_inc(S["weights"], 16)
                sp.dma_start(wv[:], A[pre + "wv"]).then_inc(S["weights"], 16)
                sp.dma_start(wo[:], A[pre + "wo"]).then_inc(S["weights"], 16)
                r = A[pre + "router"]
                sp.dma_start(wr[:, 0:r.shape[1]], r).then_inc(S["weights"], 16)
                sp.dma_start(brow[:, 0, :], A[pre + "bo"].rearrange("(a n) -> a n", a=1).to_broadcast([P, P])).then_inc(S["weights"], 16)
                if L == 0:
                    sp.dma_start(brow[:, 1, 0:E0], A["L0_ffn_gate_bias"].rearrange("(a n) -> a n", a=1).to_broadcast([P, E0])).then_inc(S["weights"], 16)
                else:
                    sp.dma_start(brow[:, 1, :], A["L1_bv"].rearrange("(a n) -> a n", a=1).to_broadcast([P, P])).then_inc(S["weights"], 16)
                    sp.dma_start(bcol[:, 0:1], A["L1_bq"].rearrange("(n a) -> n a", a=1)).then_inc(S["weights"], 16)
                    sp.dma_start(bcol[:, 1:2], A["L1_bk"].rearrange("(n a) -> n a", a=1)).then_inc(S["weights"], 16)

            def load_x(first_part, last_part):
                tiles = TOK // P // 4
                for t in range(first_part * tiles, last_part * tiles, tiles):
                    sp.dma_start(x[:, t * P:(t + tiles) * P].rearrange("p (t d) -> p t d", d=P),
                                 x_dram[:, t:t + tiles, :]).then_inc(s_x[t // tiles], 16)

            def load_mixture(L):
                part = CHUNKS[L] * CW[L] // 8
                for i in range(8):
                    sp.wait_ge(layers[L]["vp"], i + 1)
                    sp.dma_start(weights[:, i * part:(i + 1) * part], A[f"mix{L}"][:, i * part:(i + 1) * part]).then_inc(s_ffw, 16)

            load_x(0, 1)
            small(0, layers[0])
            load_x(1, 4)
            load_mixture(0)
            sp.wait_ge(layers[0]["rt"], GROUPS)
            sp.wait_ge(layers[0]["route_v"], GROUPS)
            small(1, layers[1])
            sp.wait_ge(layers[0]["x_done"], FGROUPS)
            load_mixture(1)
            sp.dma_start(b1[:], A["b1"]).then_inc(s_ffw, 16)
            for h in range(2):
                sp.dma_start(b2[h * E1:(h + 1) * E1, :], A["L1_ffn_b2"]).then_inc(s_ffw, 16)
            tiles = FTOK // P
            for g in range(FGROUPS):
                sp.wait_ge(layers[1]["x_done"], g + 1)
                sp.dma_start(out_dram[:, g * tiles:(g + 1) * tiles, :],
                             x[:, g * FTOK:(g + 1) * FTOK].rearrange("p (t d) -> p t d", d=P)).then_inc(s_out, 16)
            sp.wait_ge(s_out, FGROUPS * 16)

        N_SMALL = [9 * 16, 9 * 16]
        N_MIX = [8 * 16, (8 + 8 + 3) * 16]

        @block.tensor
        def _(pe):
            ident = cst[:, C_ID:C_ID + P]

            def attention(L):
                S = layers[L]
                pe.wait_ge(s_setup, 3)
                pe.wait_ge(S["weights"], N_SMALL[L])
                if L:
                    pe.wait_ge(layers[0]["x_done"], FGROUPS)

                def step(j, par, n, f, m, v, b, c, r, k):
                    F, M, V, B, C, K = j - 1, j - 2, j - 3, j - 4, j - 5, j - 7
                    odd = 1 - par
                    E = (E0, E1)[L]

                    def peeled(*js):
                        return isinstance(j, int) and j in js

                    def scores(u, half):
                        if u == 0 and half == 0:
                            pe.wait_ge(S["q_done"], M + 1)
                            pe.wait_ge(S["k_masked"], M + 1)
                        if half == 0 and not first(M, 0):
                            pe.wait_ge(S["probs"], M * 4 + (u - 3))
                        rows = slice(32 * u, 32 * u + 32)
                        for bb in range(half * 2, half * 2 + 2):
                            out = score[u][bb % 2 * SEQ:(bb % 2 + 1) * SEQ, half * 256:(half + 1) * 256]
                            mm = pe.matmul(out, qT[rows, par, bb * SEQ:(bb + 1) * SEQ], km[rows, par, bb, :, :],
                                           start=half == 0, stop=False, skip_group_check=True)
                        if L == 0 and half:
                            mm = pe.matmul(score[u][:, :], idb[:], band[:].unsqueeze(1).to_broadcast([P, 8, 64]),
                                           start=False, stop=False, skip_group_check=True)
                        if half:
                            mm.then_inc(S["scores"], 1)

                    def shift(u):
                        pe.wait_ge(S["max_done"], M * 4 + (u + 1))
                        pe.matmul(score[u][:, :], idr[:], nmax[:, u, :].unsqueeze(2).to_broadcast([P, 8, 64]),
                                  start=False, stop=True, skip_group_check=True).then_inc(S["shifted"], 1)

                    def turn(u):
                        pe.wait_ge(S["probs"], V * 4 + (u + 1))
                        w = (w0, w3, w3, w3)[u]
                        if u == 0 and not (isinstance(j, int) and j < LAGS):
                            pe.wait_ge(S["rt_copied"], K)
                        elif u == 0:
                            pe.wait_ge(S["q_read"], j - 1)
                        for bb in range(GB):
                            mm = pe.transpose(w[:, bb * P:(bb + 1) * P], work[:, u, bb * P:(bb + 1) * P], ident)
                        mm.then_inc(S["pt"], 1)

                    def values(u):
                        pe.wait_ge(S["pt_copied"], V * 4 + (u + 1))
                        if u == 0:
                            pe.wait_ge(S["v_done" if L else "v_masked"], V + 1)
                        if not (u == 0 and first(V, 0)):
                            pe.wait_ge(S["o_done"], V * 4 + u)
                        for pair in range(4):
                            h = u * 4 + pair % 2 * 2
                            for b2 in range(2):
                                mm = pe.matmul(w2[b2 * SEQ:(b2 + 1) * SEQ, pair * 2 * VW:(pair + 1) * 2 * VW],
                                               work2[:, u % 2, pair * P + b2 * SEQ:pair * P + (b2 + 1) * SEQ],
                                               vm[:, odd, pair // 2 * 2 + b2, h:h + 2, :], start=True, stop=True,
                                               skip_group_check=True)
                        mm.then_inc(S["op"], 1)

                    def turn_x():
                        pe.wait_ge(S["xn"], F + 1)
                        if not v and not first(F, 0):
                            pe.wait_ge(S["q_read"], F)
                        for t in range(2):
                            mm = pe.transpose(w0[:, t * P:(t + 1) * P], xn[:, odd, t, :], ident)
                        mm.then_inc(S["xt"], 1)

                    def project(n, w, rhs, done):
                        for h in range(2 - L):
                            mm = pe.matmul(w[:, h * GTOK:(h + 1) * GTOK], wqk[:, n, h * P:(h + 1) * P], rhs,
                                           start=True, stop=True)
                        mm.then_inc(done, 1)

                    def project_k():
                        pe.wait_ge(S["ctx"][odd], (F - odd) * 8 + 16)
                        pe.wait_ge(S["xt_copied"], F + 1)
                        project(1, w0, ctxT[:, odd, :, 0, :], S["kp"])

                    def project_q():
                        pe.wait_ge(S["k_read"], F + 1)
                        project(0, w0, xnT[:, odd, :], S["qp"])

                    def project_v():
                        if c:
                            pe.wait_ge(S["lg_read"], C + 1)
                        elif b:
                            pe.wait_ge(S["resid"], B + 1)
                        elif not first(F, 0):
                            pe.wait_ge(S["v_masked"], F)
                        for bb in range(GB):
                            mm = pe.matmul(w1[:, bb * P:(bb + 1) * P], ctxT[:, odd, bb, :, :], wv[:], start=True, stop=True)
                        mm.then_inc(S["vp"], 1)

                    def back_attn():
                        pe.wait_ge(S["o_done"], B * 4 + 4)
                        if peeled(GROUPS + 2, GROUPS + 3):
                            pe.wait_ge(S["lg_read"], C)
                        else:
                            pe.wait_ge(S["v_masked"], j - 1)
                        for t in range(2):
                            mm = pe.transpose(w1[:, t * P:(t + 1) * P], on[:, par, t, :], ident)
                        mm.then_inc(S["at"], 1)

                    def back_out():
                        pe.wait_ge(S["at_copied"], B + 1)
                        for t in range(2):
                            mm = pe.matmul(w1[:, t * P:(t + 1) * P], aT[:, t * P:(t + 1) * P], wo[:], start=True, stop=True)
                        mm.then_inc(S["y"], 1)

                    def back_turn():
                        pe.wait_ge(S["xn2"], C + 1)
                        if b:
                            pe.wait_ge(S["resid"], B + 1)
                        else:
                            pe.wait_ge(S["lg_read"], C)
                        for t in range(2):
                            mm = pe.transpose(w1[:, t * P:(t + 1) * P], xn2[:, t, :], ident)
                        mm.then_inc(S["x2t"], 1)

                    def back_logits():
                        pe.wait_ge(S["x2t_copied"], C + 1)
                        for t in range(2):
                            mm = pe.matmul(w1[:, t * E:(t + 1) * E], ysb[:, t * P:(t + 1) * P], wr[:, 0:E], start=True, stop=True)
                        mm.then_inc(S["lg"], 1)

                    def back_weights():
                        pe.wait_ge(S["route_v"], K + 1)
                        w = w3 if peeled(*LATE) else w0
                        if f:
                            pe.wait_ge(S["q_read"], F + 1)
                        elif not v:
                            pe.wait_ge(S["rt_copied"], K)
                        for t in range(2):
                            mm = pe.transpose(w[0:2 * E, t * P:(t + 1) * P], rw[:, t * 2 * E:(t + 1) * 2 * E], ident)
                        mm.then_inc(S["rt"], 1)

                    if m: scores(0, 0)
                    if v: turn(0)
                    if m: scores(0, 1)
                    if b: back_attn()
                    if m: scores(1, 0)
                    if v: values(0); turn(1)
                    if m: scores(1, 1)
                    if m: shift(0)
                    if b: back_out()
                    if m: scores(2, 0)
                    if f: turn_x()
                    if m: scores(2, 1)
                    if v: values(1); turn(2)
                    if m: shift(1); scores(3, 0)
                    if f: project_k()
                    if m: scores(3, 1)
                    if v: values(2)
                    if c: back_turn()
                    if v: turn(3)
                    if m: shift(2)
                    if f: project_q()
                    if c: back_logits()
                    if v: values(3)
                    if m: shift(3)
                    if k: back_weights()
                    if f: project_v()

                slots(pe, step)
                return step

            def mixture(L, step):
                S = layers[L]
                chunks, routed, lag = CHUNKS[L], ROUTED[L], DLAG[L]
                pe.wait_ge(s_ffw, N_MIX[L])
                pe.wait_ge(s_sel, 16 * (L + 1))
                pe.wait_ge(S["x2_kept"], GROUPS)
                pe.wait_ge(S["rt_copied"], GROUPS - 2)
                pe.wait_ge(S["x2t_copied"], GROUPS)
                pe.wait_ge(S["o_done"], GROUPS * 4)

                def split_product(out, w, x, start, stop):
                    (wh, wl), (xh, xl) = w, x
                    pe.matmul(out, wh, xh, start=start, stop=False, skip_group_check=True)
                    pe.matmul(out, wh, xl, start=False, stop=False, skip_group_check=True)
                    return pe.matmul(out, wl, xh, start=False, stop=stop, skip_group_check=True)

                def parts(c, column):
                    return [wsplits[L][:, c % RING[L], a, column * P:(column + 1) * P] for a in range(2)]

                def down(g, c, ring):
                    pe.wait_ge(S["h_lo"], g * chunks + (c + 1))
                    if c == 0:
                        if not first(g, 0):
                            pe.wait_ge(S["y_copied"], g)
                        if L:
                            pe.matmul(bank[6][:, :], b2[:], xin[0:2 * E1, ring, 2, :].bitcast(F32), start=True, stop=False,
                                      skip_group_check=True)
                    slot = ring * chunks + c
                    split_product(bank[6][:, :], parts(slot, 2 - L), [hsplit[:, c % 2, a, :] for a in range(2)],
                                  c == 0 and L == 0, c == chunks - 1).then_inc(S["down"], 1)

                def turn_back(g):
                    pe.wait_ge(S["y_copied"], g + 1)
                    if first(g, 0):
                        pe.wait_ge(S["rt_copied"], GROUPS)
                    if not first(g, 0):
                        pe.wait_ge(S["x_done"], g)
                    for t in range(4):
                        mm = pe.transpose(bank[7][:, t * P:(t + 1) * P], ysb[:, t * P:(t + 1) * P], cst[:, C_ID:C_ID + P])
                    mm.then_inc(S["yt"], 1)

                def group(g, u):
                    k0 = g * chunks
                    x_parts = [xin[:, u, a, :] for a in range(2)]
                    for c in range(chunks):
                        used = not first(g, 0) or c >= 2
                        slot = u * chunks + c
                        if c == 0:
                            pe.wait_ge(S["x_lo"], g + 1)
                        pe.wait_ge(S["w_lo"], k0 + (c + 1))
                        if used:
                            pe.wait_ge(S["act"], k0 + (c - 1))
                        split_product(bank[c % 2][:, :], parts(slot, 0), x_parts, True, True).then_inc(S["gate"], 1)
                        if L == 0:
                            if used:
                                pe.wait_ge(S["prod"], k0 + (c - 1))
                            split_product(bank[2 + c % 2][:, :], parts(slot, 1), x_parts, True, True).then_inc(S["up"], 1)
                        if c < routed:
                            if used:
                                pe.wait_ge(S["hid"], k0 + (c - 1))
                            if L == 0:
                                strip = slice(c // (routed // 4) * 32, c // (routed // 4) * 32 + 32)
                                cols = c % (routed // 4) * P
                            else:
                                strip, cols = slice(0, 2 * E1), c // (F1 // P) * P
                            pe.matmul(bank[4 + c % 2][:, :], sel[strip, cols:cols + P], xin[strip, u, 2, :],
                                      start=True, stop=True).then_inc(S["spread"], 1)
                        if c >= lag:
                            down(g, c - lag, u)
                        elif not first(g, 0):
                            down(g - 1, chunks - lag + c, 1 - u)
                        if first(g, 0) and c in (10, 16):
                            late(step, c == 16)
                        if c == lag + 1 and not first(g, 0):
                            turn_back(g - 1)

                pairs(pe, group)
                for c in range(chunks - lag, chunks):
                    down(FGROUPS - 1, c, 1)
                turn_back(FGROUPS - 1)

            for L in range(2):
                mixture(L, attention(L))

        @block.scalar
        def _(act):
            for L in range(2):
                S = layers[L]
                E = (E0, E1)[L]

                def load_context(j, par):
                    act.dma_start(arena[:, par * 2 * GTOK:(par + 1) * 2 * GTOK],
                                  A["ctxT"][:, bass.ds(j * 2 * GTOK, 2 * GTOK)]).then_inc(S["ctx"][par], 16)

                if L:
                    act.wait_ge(layers[0]["x_done"], FGROUPS)
                load_context(0, 0)
                if L == 0:
                    act.wait_ge(S["weights"], N_SMALL[L])
                    act.activation(gates[:], gates[:], ACT.Tanh).then_inc(S["tanh"], 1)
                scale = (HD ** 0.5, HD ** -0.5)[L]

                def step(j, par, n, f, m, v, b, c, r, k):
                    F, M, V, B, C, K = j - 1, j - 2, j - 3, j - 4, j - 5, j - 7
                    odd = 1 - par

                    def copy_turned(u):
                        act.wait_ge(S["pt"], V * 4 + (u + 1))
                        act.activation(work2[:, u % 2, :], (w0, w3, w3, w3)[u][:, :], ACT.Copy).then_inc(S["pt_copied"], 1)

                    def exps(u):
                        act.wait_ge(S["shifted"], M * 4 + (u + 1))
                        act.activation(work[:, u, :], score[u][:, :], ACT.Exp, scale=scale).then_inc(S["probs"], 1)

                    def keep_weights():
                        act.wait_ge(S["rt"], K + 1)
                        w = w3 if first(j, LATE[0]) or first(j, LATE[1]) else w0
                        act.activation(rwT[0:2 * E, bass.ds(K * GTOK, GTOK)], w[0:2 * E, 0:GTOK], ACT.Copy).then_inc(S["rt_copied"], 1)

                    def copy_attn():
                        act.wait_ge(S["at"], B + 1)
                        act.activation(aT[:], w1[:, 0:GTOK], ACT.Copy).then_inc(S["at_copied"], 1)

                    def copy_xn():
                        act.wait_ge(S["xt"], F + 1)
                        act.activation(xnT[:, odd, :], w0[:, 0:GTOK], ACT.Copy).then_inc(S["xt_copied"], 1)

                    def copy_xn2():
                        if isinstance(C, int) and C > 0:
                            act.wait_ge(S["x2_kept"], C)
                        act.wait_ge(S["x2t"], C + 1)
                        act.activation(ysb[:, 0:GTOK], w1[:, 0:GTOK], ACT.Copy).then_inc(S["x2t_copied"], 1)

                    def mask_keys():
                        if L == 0:
                            act.wait_ge(S["k_roped"], F + 1)
                        else:
                            act.wait_ge(S["kp"], F + 1)
                            if first(F, 0):
                                act.wait_ge(S["prep"], 1)
                        for h in range(4):
                            if L == 0:
                                a = act.activation(km[:, odd, :, h, :], kr[:].rearrange("p (b s) -> p b s", s=SEQ), ACT.Copy,
                                                   scale=cst[:, C_HM + h:C_HM + h + 1])
                            else:
                                a = act.activation(km[:, odd, :, h, :], w0[:, 0:GTOK].rearrange("p (b s) -> p b s", s=SEQ), ACT.Identity,
                                                   bias=bk4[:, h:h + 1], scale=cst[:, C_HM + h:C_HM + h + 1])
                        a.then_inc(S["k_masked"], 1)

                    def read_logits():
                        if L == 1 and not first(C, 0):
                            act.wait_ge(S["p2v"], C)
                        act.wait_ge(S["lg"], C + 1)
                        if L == 0:
                            act.activation(sg[:], w1[:, 0:2 * E0], ACT.Exp, scale=-1.0).then_inc(S["lg_read"], 1)
                        else:
                            act.activation(sg[:, 0:2 * E1], w1[:, 0:2 * E1], ACT.Copy).then_inc(S["lg_read"], 1)

                    def keep_xn2():
                        act.wait_ge(S["x2t_copied"], C + 1)
                        act.activation(xn2T[:, bass.ds(C * GTOK, GTOK)], ysb[:, 0:GTOK], ACT.Copy).then_inc(S["x2_kept"], 1)

                    if n and not first(j, 0):
                        if not first(j, 1):
                            act.wait_ge(S["vp"], j - 1)
                        load_context(j, par)
                    if v: copy_turned(0)
                    if b: copy_attn()
                    if v: copy_turned(1)
                    if m: exps(0)
                    if f: copy_xn()
                    if v: copy_turned(2)
                    if m: exps(1)
                    if f and L == 1: mask_keys()
                    if c: copy_xn2()
                    if v: copy_turned(3)
                    if m: exps(2)
                    if c: read_logits(); keep_xn2()
                    if f and L == 0: mask_keys()
                    if k: keep_weights()
                    if m: exps(3)
                    if c and L == 1:
                        act.wait_ge(S["v2a"], C + 1)
                        act.activation(sc[:, 0:2 * E1], choice[:, 0:2 * E1], ACT.Exp).then_inc(S["a2v"], 1)

                slots(act, step)

                chunks = CHUNKS[L]
                last = FGROUPS * chunks

                act.wait_ge(s_ffw, N_MIX[L])
                act.wait_ge(S["x2_kept"], GROUPS)
                act.wait_ge(S["rt_copied"], GROUPS - 2)
                act.wait_ge(S["at"], GROUPS)
                act.wait_ge(S["lg"], GROUPS)

                def split_input(g, u):
                    if not (first(g, 0) or first(g, 1)):
                        act.wait_ge(S["down"], (g - 1) * chunks)
                    act.activation(xin[:, u, 0, :], xn2T[:, bass.ds(g * FTOK, FTOK)], ACT.Copy).then_inc(S["x_hi"], 1)
                    act.activation(xin[0:2 * E, u, 2, :], rwT[0:2 * E, bass.ds(g * FTOK, FTOK)].bitcast(F32), ACT.Copy).then_inc(S["x_hi"], 1)

                def split_weights(n, c, slot):
                    if not (isinstance(n, int) and n < RING[L]):
                        act.wait_ge(S["down"], n - (RING[L] - 1))
                    act.activation(wsplits[L][:, slot % RING[L], 0, 0:CW[L]], weights[:, c * CW[L]:(c + 1) * CW[L]],
                                   ACT.Copy).then_inc(S["w_hi"], 1)

                def split_hidden(n, c):
                    act.wait_ge(S["hid"], n + 1)
                    if not (isinstance(n, int) and n < 2):
                        act.wait_ge(S["down"], n - 1)
                    act.activation(hsplit[:, c % 2, 0, :], work2[:, c % 2, :], ACT.Copy).then_inc(S["h_hi"], 1)

                def copy_sum(g):
                    act.wait_ge(S["down"], (g + 1) * chunks)
                    if not first(g, 0):
                        act.wait_ge(S["yt"], g)
                    act.activation(ysb[:], bank[6][:, :], ACT.Copy).then_inc(S["y_copied"], 1)

                def group(g, u):
                    k0 = g * chunks
                    if first(g, 0):
                        split_input(g, u)
                        for c in range(AHEAD[L]):
                            split_weights(c, c, c)
                    for c in range(chunks):
                        if c + AHEAD[L] < chunks or not first(g, FGROUPS - 1):
                            split_weights(k0 + (c + AHEAD[L]), (c + AHEAD[L]) % chunks, u * chunks + c + AHEAD[L])
                        if c == DLAG[L] and not first(g, 0):
                            copy_sum(g - 1)
                        act.wait_ge(S["gate"], k0 + (c + 1))
                        if not first(g, 0) or c >= 2:
                            act.wait_ge(S["hid" if L else "prod"], k0 + (c - 1))
                        if L == 0:
                            act.activation(work[:, c % 2, :], bank[c % 2][:, :], ACT.Silu).then_inc(S["act"], 1)
                        else:
                            act.activation(work[:, c % 2, :], bank[c % 2][:, :], ACT.Gelu_apprx_tanh,
                                           bias=b1[:, c:c + 1]).then_inc(S["act"], 1)
                        if not first(g, 0) or c >= 1:
                            split_hidden(k0 + (c - 1), c - 1)
                        if first(g, 0) and c in (11, 17):
                            late(step, c == 17)
                        if c == chunks // 2 and not first(g, FGROUPS - 1):
                            split_input(g + 1, 1 - u)

                pairs(act, group)
                split_hidden(last - 1, chunks - 1)
                copy_sum(FGROUPS - 1)

        @block.vector
        def _(dve):
            dve.wait_ge(s_const, 16)
            dve.tensor_copy(idr[:], cst[:, C_ID:C_ID + P]).then_inc(s_setup, 1)
            dve.tensor_copy(idb[:], cst[:, C_ID:C_ID + P]).then_inc(s_setup, 1)
            dve.tensor_copy(band[:], cst[:, C_BAND:C_BAND + 64]).then_inc(s_setup, 1)
            dve.tensor_copy(vm[:].rearrange("p a b h x -> p (a b h) x")[:, :, HD].rearrange("p (n t) -> p n t", t=2),
                            cst[:, C_JM:C_JM + 2].unsqueeze(1).to_broadcast([P, GB * HEADS, 2]))

            for L in range(2):
                S = layers[L]
                E = (E0, E1)[L]
                if L == 0:
                    dve.wait_ge(S["tanh"], 1)
                else:
                    dve.wait_ge(S["weights"], N_SMALL[L])
                dve.tensor_scalar(gbo[:], brow[:, 0, :], gates[:, L:L + 1], None, ALU.mult)
                if L:
                    dve.tensor_tensor(bvm[:].rearrange("p (n t d) -> p n t d", t=2, d=HD),
                                      brow[:, 1, :].rearrange("p (n t d) -> p n t d", t=2, d=HD),
                                      cst[:, C_JM:C_JM + 2].unsqueeze(1).unsqueeze(3).to_broadcast([P, 8, 2, HD]), ALU.mult)
                dve.tensor_scalar(bk4[:], cst[:, C_HM:C_HM + 4], bcol[:, 1:2] if L else 0.0, None, ALU.mult).then_inc(S["prep"], 1)

                def step(j, par, n, f, m, v, b, c, r, k):
                    F, M, V, B, C, R = j - 1, j - 2, j - 3, j - 4, j - 5, j - 6
                    odd = 1 - par

                    def norm_stats():
                        if L == 0 and (first(j, 0) or first(j, 4)):
                            dve.wait_ge(s_x[j // 4], 16)
                        if L == 0 and first(j, LAGS - 1):
                            dve.wait_ge(s_x[2], 16)
                            dve.wait_ge(s_x[3], 16)
                        for t in range(2):
                            a = dve.bn_stats(st[:, par, t, :], x[:, bass.ds(j * GTOK + t * P, P)])
                        a.then_inc(S["stats"], 1)
                        hold(dve, S["stats"], j + 1)
                        for t in range(2):
                            a = dve.bn_aggr(mv[:, par, t, :], st[:, par, t, :])
                        a.then_inc(S["varp"], 1)

                    def norm_apply():
                        dve.wait_ge(S["rstd"], j * 2 + 2)
                        for t in range(2):
                            a = dve.tensor_scalar(xn[:, par, t, :], x[:, bass.ds(j * GTOK + t * P, P)],
                                                  mv[:, par, t, 0:1], rs[:, par, t:t + 1], ALU.subtract, ALU.mult)
                        a.then_inc(S["xn"], 1)

                    def max_rows(u):
                        dve.wait_ge(S["scores"], M * 4 + (u + 1))
                        dve.tensor_reduce(nmax[:, u, :], score[u][:].rearrange("p (a k) -> p a k", k=SEQ), AX.X, ALU.max,
                                          negate=True).then_inc(S["max_done"], 1)

                    def outs(u):
                        dve.wait_ge(S["op"], V * 4 + (u + 1))
                        o = w2[:, 0:8 * VW].rearrange("p (t h x) -> p t h x", t=2, x=VW)
                        dve.reciprocal(rden[:, odd, :, :], o[:, :, :, HD]).then_inc(S["rden"], 1)
                        dve.wait_ge(S["rden"], V * 4 + (u + 1))
                        dve.tensor_tensor(on[:, odd, :, 32 * u:32 * u + 32].rearrange("p t (h d) -> p t h d", d=HD),
                                          o[:, :, :, 0:HD], rden[:, odd, :, :].unsqueeze(3).to_broadcast([P, 2, 4, HD]),
                                          ALU.mult).then_inc(S["o_done"], 1)

                    def rotate(n, w, ready, read):
                        dve.wait_ge(ready, F + 1)
                        if not first(F, 0):
                            dve.wait_ge(S[("k_roped", "q_done")[n]], F)
                        for h in range(2):
                            a = dve.tensor_tensor(rope[:, 2 * n + h, :].rearrange("p (b s) -> p b s", s=SEQ),
                                                  w[:, h * GTOK:(h + 1) * GTOK].rearrange("p (b s) -> p b s", s=SEQ),
                                                  cst[:, C_COS + 64 * h:C_COS + 64 * h + 64].unsqueeze(1).to_broadcast([P, GB, 64]),
                                                  ALU.mult)
                        a.then_inc(read, 1)

                    def mask_values():
                        dve.wait_ge(S["vp"], F + 1)
                        dve.tensor_tensor(vm[:, odd, :, :, 0:HD].rearrange("p b (n t) d -> p (b n) t d", t=2),
                                          w1[:].rearrange("p (n t d) -> p n t d", t=2, d=HD),
                                          cst[:, C_JM:C_JM + 2].unsqueeze(1).unsqueeze(3).to_broadcast([P, GB * 8, 2, HD]),
                                          ALU.mult).then_inc(S["v_masked"], 1)

                    def residual():
                        dve.wait_ge(S["y"], B + 1)
                        dve.wait_ge(S["xb"], B + 1)
                        xs = x[:, bass.ds(B * GTOK, GTOK)]
                        dve.scalar_tensor_tensor(xs, w1[:, 0:GTOK], gates[:, L:L + 1], xb[:, par, :], ALU.mult, ALU.add).then_inc(S["resid"], 1)
                        hold(dve, S["resid"], B + 1)
                        for t in range(2):
                            a = dve.bn_stats(st2[:, t, :], x[:, bass.ds(B * GTOK + t * P, P)])
                        a.then_inc(S["stats2"], 1)
                        hold(dve, S["stats2"], B + 1)
                        for t in range(2):
                            a = dve.bn_aggr(mv2[:, par, t, :], st2[:, t, :])
                        a.then_inc(S["varp2"], 1)

                    def norm2_apply():
                        dve.wait_ge(S["rstd2"], C * 2 + 2)
                        for t in range(2):
                            a = dve.tensor_scalar(xn2[:, t, :], x[:, bass.ds(C * GTOK + t * P, P)],
                                                  mv2[:, odd, t, 0:1], rs2[:, odd, t:t + 1], ALU.subtract, ALU.mult)
                        a.then_inc(S["xn2"], 1)

                    def score_one():
                        dve.wait_ge(S["lg_read"], C + 1)
                        dve.tensor_scalar(sc[:], sg[:], 1.0, None, ALU.add).then_inc(S["v2a"], 1)

                    def score_two():
                        dve.wait_ge(S["v2a"], C * 3 + 1)
                        dve.reciprocal(sc[:], sc[:]).then_inc(S["v2a"], 1)

                    def score_three():
                        dve.wait_ge(S["v2a"], C * 3 + 2)
                        dve.tensor_tensor(choice[:].rearrange("p (t e) -> p t e", e=E0), sc[:].rearrange("p (t e) -> p t e", e=E0),
                                          brow[:, 1, 0:E0].unsqueeze(1).to_broadcast([P, 2, E0]), ALU.add).then_inc(S["v2a"], 1)

                    def score_four():
                        hold(dve, S["v2a"], C * 3 + 3)
                        for g in range(16):
                            a = dve.max(gtop[:, g, :], choice[:, g * 8:(g + 1) * 8])
                        a.then_inc(S["v2p"], 1)

                    def score_logits():
                        lg = sg[:, 0:2 * E1].rearrange("p (t e) -> p t e", e=E1)
                        dve.wait_ge(S["lg_read"], C + 1)
                        dve.tensor_reduce(top8[:, 0, 0:2], lg, AX.X, ALU.max).then_inc(S["v2p"], 1)
                        dve.wait_ge(S["v2p"], C + 1)
                        dve.tensor_tensor(choice[:, 0:2 * E1].rearrange("p (t e) -> p t e", e=E1), lg,
                                          top8[:, 0, 0:2].unsqueeze(2).to_broadcast([P, 2, E1]), ALU.subtract).then_inc(S["v2a"], 1)

                    ws = wsel[:, 0:2 * E]
                    wt = ws.rearrange("p (t e) -> p t e", e=E)
                    kept = rwr[:, 0:2 * E]
                    links = (8, 5)[L]

                    def pick_one():
                        hold(dve, S["p2v"], R + 1)
                        for t in range(2):
                            a = dve.max(top8[:, t, :], masked[:, t * E:(t + 1) * E])
                        a.then_inc(S["chain"], 1)

                    def pick_two():
                        hold(dve, S["chain"], R * links + 1)
                        for t in range(2):
                            a = dve.match_replace(rest[:, t * E:(t + 1) * E], top8[:, t, :], masked[:, t * E:(t + 1) * E], MASKED)
                        a.then_inc(S["chain"], 1)

                    def pick_three():
                        dve.wait_ge(S["chain"], R * links + 2)
                        dve.scalar_tensor_tensor(ws, rest[:], MASKED * 0.5, sc[:], ALU.is_lt, ALU.mult).then_inc(S["chain"], 1)

                    def pick_best_two():
                        dve.wait_ge(S["a2v"], R + 1)
                        dve.wait_ge(S["p2v"], R + 1)
                        dve.tensor_tensor(ws, sc[:, 0:2 * E], masked[:, 0:2 * E], ALU.mult).then_inc(S["chain"], 1)

                    def weigh_one():
                        dve.wait_ge(S["chain"], R * links + links - 4 - (L == 0))
                        dve.tensor_reduce(wsum[:], wt, AX.X, ALU.add).then_inc(S["chain"], 1)

                    def weigh_two():
                        if L == 0:
                            dve.wait_ge(S["chain"], R * links + links - 4)
                            dve.tensor_scalar(wsum[:], wsum[:], 1e-20, None, ALU.add).then_inc(S["chain"], 1)

                    def weigh_three():
                        dve.wait_ge(S["chain"], R * links + links - 3)
                        dve.reciprocal(wsum[:], wsum[:]).then_inc(S["chain"], 1)

                    def weigh_four():
                        hold(dve, S["chain"], R * links + links - 2)
                        dve.scalar_tensor_tensor(wt, wt, (RSCALE, 1.0)[L], wsum[:].unsqueeze(2).to_broadcast([P, 2, E]),
                                                 ALU.mult, ALU.mult).then_inc(S["chain"], 1)

                    def weigh_five():
                        dve.wait_ge(S["chain"], R * links + links - 1)
                        dve.tensor_copy(kept, ws).then_inc(S["chain"], 1)

                    def weigh_six():
                        strip = (STRIP_E, E1)[L]
                        parts = rw[:, 0:4 * E].rearrange("p (t a e) -> p t a e", a=2, e=strip)
                        dve.wait_ge(S["chain"], R * links + links)
                        if not first(R, 0):
                            dve.wait_ge(S["rt"], R)
                        dve.tensor_copy(parts[:, :, 0, :], kept.bitcast(F32).rearrange("p (t e) -> p t e", e=strip))
                        dve.tensor_tensor(parts[:, :, 1, :], ws.rearrange("p (t e) -> p t e", e=strip),
                                          kept.bitcast(F32).rearrange("p (t e) -> p t e", e=strip),
                                          ALU.subtract).then_inc(S["route_v"], 1)

                    def bias_queries():
                        dve.wait_ge(S["qp"], F + 1)
                        dve.tensor_scalar(qT[:, odd, :], w0[:, 0:GTOK], bcol[:, 0:1], None, ALU.add).then_inc(S["q_done"], 1)

                    if c: norm2_apply()
                    if m: max_rows(0)
                    if n: norm_stats()
                    if m: max_rows(1)
                    if v: outs(0)
                    if b: residual()
                    if m: max_rows(2)
                    if v: outs(1)
                    if r and L == 0: pick_one()
                    if f and L == 0: rotate(0, w0, S["kp"], S["k_read"])
                    if r and L == 0: pick_two()
                    if m: max_rows(3)
                    if r and L == 0: pick_three()
                    if r and L == 1: pick_best_two()
                    if v: outs(2)
                    if r: weigh_one()
                    if f and L == 0: rotate(1, w0, S["qp"], S["q_read"])
                    if f and L == 1: bias_queries()
                    if r: weigh_two()
                    if c and L == 0: score_one()
                    if c and L == 1: score_logits()
                    if r: weigh_three()
                    if v: outs(3)
                    if r: weigh_four()
                    if c and L == 0: score_two()
                    if r: weigh_five()
                    if f: mask_values()
                    if r: weigh_six()
                    if c and L == 0: score_three()
                    if n: norm_apply()
                    if c and L == 0: score_four()

                slots(dve, step)

                chunks, routed = CHUNKS[L], ROUTED[L]
                dve.wait_ge(S["pt_copied"], GROUPS * 4)

                def split_input(g, u):
                    dve.wait_ge(S["x_hi"], g * 2 + 2)
                    dve.tensor_tensor(xin[:, u, 1, :], xn2T[:, bass.ds(g * FTOK, FTOK)], xin[:, u, 0, :].bitcast(F32),
                                      ALU.subtract).then_inc(S["x_lo"], 1)

                def split_hidden(n, c):
                    dve.wait_ge(S["h_hi"], n + 1)
                    dve.tensor_tensor(hsplit[:, c % 2, 1, :], work2[:, c % 2, :], hsplit[:, c % 2, 0, :].bitcast(F32),
                                      ALU.subtract).then_inc(S["h_lo"], 1)

                def add_sum(g):
                    dve.wait_ge(S["yt"], g + 1)
                    xs = x[:, bass.ds(g * FTOK, FTOK)]
                    dve.scalar_tensor_tensor(xs, bank[7][:, :], gates[:, 2 + L:3 + L], xs, ALU.mult, ALU.add).then_inc(S["x_done"], 1)

                def group(g, u):
                    k0 = g * chunks
                    if first(g, 0):
                        split_input(g, u)
                    for c in range(chunks):
                        held = work2[:, c % 2, :]
                        used_before = not first(g, 0) or c >= 1
                        if L == 0:
                            dve.wait_ge(S["act"], k0 + (c + 1))
                            dve.wait_ge(S["up"], k0 + (c + 1))
                            dve.tensor_tensor(work[:, 2 + c % 2, :], work[:, c % 2, :], bank[2 + c % 2][:, :],
                                              ALU.mult).then_inc(S["prod"], 1)
                        if L == 0 and used_before:
                            split_hidden(k0 + (c - 1), c - 1)
                        dve.wait_ge(S["act" if L else "prod"], k0 + (c + 1))
                        if not first(g, 0) or c >= 2:
                            dve.wait_ge(S["h_lo"], k0 + (c - 1))
                        if c < routed:
                            dve.wait_ge(S["spread"], g * routed + (c + 1))
                            dve.tensor_tensor(held, work[:, (2 + c % 2, c % 2)[L], :], bank[4 + c % 2][:, :],
                                              ALU.mult).then_inc(S["hid"], 1)
                        else:
                            dve.tensor_copy(held, work[:, 2 + c % 2, :]).then_inc(S["hid"], 1)
                        if L and used_before:
                            split_hidden(k0 + (c - 1), c - 1)
                        if c == 5 and not first(g, 0):
                            add_sum(g - 1)
                        if first(g, 0) and c == 10:
                            late(step, 0)
                        if c == chunks // 2 and not first(g, FGROUPS - 1):
                            split_input(g + 1, 1 - u)

                pairs(dve, group)
                split_hidden(FGROUPS * chunks - 1, chunks - 1)
                add_sum(FGROUPS - 1)
                dve.wait_ge(S["x_done"], FGROUPS)

        @block.gpsimd
        def _(pool):
            pool.memset(mhalf[:], -0.5).then_inc(s_half, 1)
            pool.dma_start(sel[:], A["sel0"]).then_inc(s_sel, 16)
            pool.wait_ge(s_half, 1)
            for L in range(2):
                S = layers[L]
                pool.wait_ge(S["prep"], 1)

                def step(j, par, n, f, m, v, b, c, r, k):
                    F, V, B, R = j - 1, j - 3, j - 4, j - 6
                    odd = 1 - par

                    def add_bias():
                        if not (first(V, 0) or first(V, 1)):
                            pool.wait_ge(S["resid"], V - 1)
                        pool.tensor_tensor(xb[:, odd, :].rearrange("p (t d) -> p t d", d=P),
                                           x[:, bass.ds(V * GTOK, GTOK)].rearrange("p (t d) -> p t d", d=P),
                                           gbo[:].unsqueeze(1).to_broadcast([P, 2, P]), ALU.add).then_inc(S["xb"], 1)

                    def deviation(varp, rstd, group, var, plus, inverse):
                        hold(pool, varp, group + 1)
                        pool.tensor_scalar(plus, var, EPS, None, ALU.add).then_inc(rstd, 1)
                        pool.wait_ge(rstd, group * 2 + 1)
                        pool.tensor_tensor(inverse, plus, mhalf[:], ALU.pow).then_inc(rstd, 1)

                    def rope_keys():
                        pool.wait_ge(S["k_read"], F + 1)
                        if not first(F, 0):
                            pool.wait_ge(S["k_masked"], F)
                        pool.tensor_tensor(kr[:], rope[:, 0, :], rope[:, 1, :], ALU.add).then_inc(S["k_roped"], 1)

                    def rope_queries():
                        pool.wait_ge(S["q_read"], F + 1)
                        pool.tensor_tensor(qT[:, odd, :], rope[:, 2, :], rope[:, 3, :], ALU.add).then_inc(S["q_done"], 1)

                    def bias_values():
                        pool.wait_ge(S["v_masked"], F + 1)
                        vals = vm[:, odd, :, :, 0:HD]
                        pool.tensor_tensor(vals, vals, bvm[:].rearrange("p (h d) -> p h d", d=HD).unsqueeze(1).to_broadcast([P, GB, HEADS, HD]),
                                           ALU.add).then_inc(S["v_done"], 1)

                    if r and L == 0:
                        pool.wait_ge(S["v2p"], R + 1)
                        route0(R)
                    if r and L == 1:
                        pool.wait_ge(S["lg_read"], R + 1)
                        route1(R)
                    if b: deviation(S["varp2"], S["rstd2"], B, mv2[:, par, :, 1], ve2[:, par, :], rs2[:, par, :])
                    if f and L == 0: rope_keys(); rope_queries()
                    if n: deviation(S["varp"], S["rstd"], j, mv[:, par, :, 1], ve[:, par, :], rs[:, par, :])
                    if v: add_bias()
                    if L and first(j, LAGS - 1):
                        pool.dma_start(sel[0:2 * E1, 0:E1 * P], A["sel1"]).then_inc(s_sel, 16)
                    if f and L == 1: bias_values()

                def ranks(link, val):
                    values = val[:, 0:16].rearrange("p (t e) -> p t e", t=2)
                    vj = values.unsqueeze(2).to_broadcast([P, 2, 8, 8])
                    vi = values.unsqueeze(3).to_broadcast([P, 2, 8, 8])
                    gt, eq = cmp[:, 0, :], cmp[:, 1, :]
                    link(pool.tensor_tensor(gt.rearrange("p (t i j) -> p t i j", i=8, j=8), vj, vi, ALU.subtract))
                    link(pool.tensor_scalar(eq, gt, 0.0, None, ALU.is_equal))
                    link(pool.tensor_scalar(gt, gt, 0.0, None, ALU.is_gt))
                    eq2 = eq.rearrange("p (t n) -> p t n", t=2)
                    link(pool.tensor_tensor(eq2, eq2, cst[:, C_TRI:C_END].unsqueeze(1).to_broadcast([P, 2, 64]), ALU.mult))
                    link(pool.tensor_tensor(cmp[:, 0, :], cmp[:, 0, :], cmp[:, 1, :], ALU.add))
                    c = cmp[:, 0, :].rearrange("p (i j) -> p i j", j=8)
                    link(pool.tensor_tensor(cmp[:, 1, 0:64].rearrange("p (i j) -> p i j", j=4), c[:, :, 0:4], c[:, :, 4:8], ALU.add))
                    c = cmp[:, 1, 0:64].rearrange("p (i j) -> p i j", j=4)
                    link(pool.tensor_tensor(cmp[:, 0, 0:32].rearrange("p (i j) -> p i j", j=2), c[:, :, 0:2], c[:, :, 2:4], ALU.add))
                    c = cmp[:, 0, 0:32].rearrange("p (i j) -> p i j", j=2)
                    link(pool.tensor_tensor(rank[:], c[:, :, 0], c[:, :, 1], ALU.add))

                def route0(B):
                    n = [0]

                    def link(ins):
                        n[0] += 1
                        ins.then_inc(S["route_p"], 1)
                        hold(pool, S["route_p"], B * 10 + n[0])
                    link(pool.tensor_tensor(gsum[:], gtop[:, :, 0], gtop[:, :, 1], ALU.add))
                    ranks(link, gsum)
                    link(pool.tensor_scalar(rank[:], rank[:], float(TOPG0), None, ALU.is_lt))
                    if not first(B, 0):
                        pool.wait_ge(S["route_v"], B)
                    pool.tensor_tensor(masked[:].rearrange("p (g e) -> p g e", e=8), choice[:].rearrange("p (g e) -> p g e", e=8),
                                       rank[:].unsqueeze(2).to_broadcast([P, 16, 8]), ALU.mult).then_inc(S["p2v"], 1)
                    assert n[0] == 10, n[0]

                def route1(B):
                    n = [0]

                    def link(ins):
                        n[0] += 1
                        ins.then_inc(S["route_p"], 1)
                        hold(pool, S["route_p"], B * 8 + n[0])
                    ranks(link, sg)
                    if not first(B, 0):
                        hold(pool, S["route_v"], B)
                    pool.tensor_scalar(masked[:, 0:16], rank[:], 2.0, None, ALU.is_lt).then_inc(S["p2v"], 1)
                    assert n[0] == 8, n[0]

                slots(pool, step)

                chunks = CHUNKS[L]

                def group(g, u):
                    for c in range(chunks):
                        if first(g, 0) and c == 2:
                            late(step, 0)
                        slot = (u * chunks + c) % RING[L]
                        pool.wait_ge(S["w_hi"], g * chunks + (c + 1))
                        pool.tensor_tensor(wsplits[L][:, slot, 1, 0:CW[L]], weights[:, c * CW[L]:(c + 1) * CW[L]],
                                           wsplits[L][:, slot, 0, 0:CW[L]].bitcast(F32), ALU.subtract).then_inc(S["w_lo"], 1)

                pairs(pool, group)


def kernel(**inputs):
    import concourse.bacc as _bacc
    from concourse.bass_utils import run_bass_kernel_spmd as _run

    I = {k: np.asarray(v) for k, v in inputs.items()}
    swap = np.concatenate([np.arange(64, 128), np.arange(0, 64)])
    a = {"cst": constants(), "x": I["x"]}
    a["sel0"], a["sel1"] = spread_rows()
    a["ctxT"] = np.repeat(I["ctx_1024"].transpose(2, 0, 1)[:, :, None], 2, axis=2).reshape(D, 2 * TOK)
    for n in ("g_xattn", "g_ffn", "L0_ffn_gate_bias", "L1_ffn_b2"):
        a[n] = I[n]
    for s in "qk":
        w = I["L0_xattn_w" + s].T
        a["L0_w" + s] = np.concatenate([w, w[:, swap]], axis=1)
        a["L1_w" + s] = I["L1_xattn_W_" + s]
    a["L0_wv"], a["L1_wv"] = I["L0_xattn_wv"].T, I["L1_xattn_W_v"]
    a["L0_wo"], a["L1_wo"] = I["L0_xattn_wo_w"].T, I["L1_xattn_W_o"]
    a["L0_bo"], a["L1_bo"] = I["L0_xattn_wo_b"], I["L1_xattn_b_o"]
    a["L1_bq"], a["L1_bk"], a["L1_bv"] = I["L1_xattn_b_q"], I["L1_xattn_b_k"], I["L1_xattn_b_v"]
    a["L0_router"], a["L1_router"] = I["L0_ffn_gate_w"].T, I["L1_ffn_Wg"]
    rows = CHUNKS[0] * P
    gate, up, down = np.zeros((3, rows, D), np.float32)
    gate[:ROUTED0], up[:ROUTED0] = I["L0_ffn_Wg"].reshape(ROUTED0, D), I["L0_ffn_Wu"].reshape(ROUTED0, D)
    gate[ROUTED0:ROUTED0 + SHARED], up[ROUTED0:ROUTED0 + SHARED] = I["L0_ffn_Sg"], I["L0_ffn_Su"]
    down[:ROUTED0] = I["L0_ffn_Wd"].transpose(0, 2, 1).reshape(ROUTED0, D)
    down[ROUTED0:ROUTED0 + SHARED] = I["L0_ffn_Sd"].T
    turned = [w.reshape(CHUNKS[0], P, D).transpose(2, 0, 1) for w in (gate, up)]
    a["mix0"] = np.concatenate(turned + [down.reshape(CHUNKS[0], P, D).transpose(1, 0, 2)], axis=2).reshape(P, -1)
    w1 = I["L1_ffn_W1"].transpose(1, 0, 2).reshape(D, CHUNKS[1], P)
    w2 = I["L1_ffn_W2"].reshape(CHUNKS[1], P, D).transpose(1, 0, 2)
    a["mix1"] = np.concatenate([w1, w2], axis=2).reshape(P, -1)
    a["b1"] = I["L1_ffn_b1"].reshape(CHUNKS[1], P).T

    nc = _bacc.Bacc("TRN2", target_bir_lowering=False, num_devices=1)
    arrays, args = {}, {}
    for name, v in a.items():
        v = np.ascontiguousarray(v)
        arrays[f"in_{name}"] = v
        args[name] = nc.dram_tensor(f"in_{name}", v.shape, mybir.dt.from_np(v.dtype), kind="ExternalInput").ap()
    out = nc.dram_tensor("out_0", (BATCH, SEQ, D), F32, kind="ExternalOutput").ap()
    build(nc, args, out)
    r = _run(nc, [arrays], core_ids=[0])
    return r.results[0]["out_0"]
```
